# Optimizing a Trainium2 kernel written in Bass

```python
import numpy as np
import jax
import jax.numpy as jnp

def _softmax(x, axis=-1):
    return jax.nn.softmax(x, axis=axis)

def _gelu(x):
    return jax.nn.gelu(x, approximate=True)

def _silu(x):
    return jax.nn.silu(x)

def _sigmoid(x):
    return jax.nn.sigmoid(x)

def _layernorm(x, axis=-1, eps=1e-05):
    m = jnp.mean(x, axis=axis, keepdims=True)
    v = jnp.var(x, axis=axis, keepdims=True)
    return (x - m) / jnp.sqrt(v + eps)

def _scatter_add(tgt, idx, src, axis=0):
    return tgt.at[idx].add(src)

def _segment_sum(src, seg, n):
    return jax.ops.segment_sum(src, seg, n)
kernel_name = 'mk_gnn_preln_d2_gnn_r32_ec8046'

def setup_inputs(seed: int=0):
    np.random.seed(seed)
    _w = jnp.asarray

    def _rec_inputs():
        import jax
        import jax.numpy as jnp
        _gk = jax.random.key(seed)
        x = -0.0005121 + 1.001 * jax.random.normal(jax.random.fold_in(_gk, 1), (3125, 32), jnp.float32)
        _s = jax.random.randint(jax.random.fold_in(_gk, 2), (25000,), 0, 3125, jnp.int32)
        _d = jax.random.randint(jax.random.fold_in(_gk, 3), (25000,), 0, 3125, jnp.int32)
        _loop = jnp.arange(3125, dtype=jnp.int32)
        src = jnp.concatenate([_s, _d, _loop])
        dst = jnp.concatenate([_d, _s, _loop])
        _o = jnp.argsort(dst, stable=True)
        src = src[_o]
        dst = dst[_o]
        edge_attr_32 = 0.000216709 + 1.00012 * jax.random.normal(jax.random.fold_in(_gk, 11), (53125, 32), jnp.float32)
        edge_attr_4 = 0.000714719 + 1.00021 * jax.random.normal(jax.random.fold_in(_gk, 12), (53125, 4), jnp.float32)
        return (x, src, dst, edge_attr_32, edge_attr_4)
    x, src, dst, edge_attr_32, edge_attr_4 = _rec_inputs()

    def _L0_gnn_setup():
        import jax, jax.numpy as jnp
        import numpy as np
        MUL = 8
        N_NODES = 3125
        N_EDGES = 25000
        EDGE_DIM = 32
        MLP_DIM = 64
        W_NUMEL = 4 * MUL * MUL
        ALPHA = 0.25
        C110 = 1.0 / np.sqrt(3.0)
        SI_SCALE = 1.0 / np.sqrt(MUL)
        key = jax.random.key(seed)
        ks = jax.random.split(key, 10)
        node_attr = jax.random.normal(ks[0], (N_NODES, 4 * MUL), dtype=jnp.float32)
        edge_index = jax.random.randint(ks[1], (2, N_EDGES), 0, N_NODES, dtype=jnp.int64)
        edge_sh = jax.random.normal(ks[2], (N_EDGES, 4), dtype=jnp.float32)
        edge_feat = jax.random.normal(ks[3], (N_EDGES, EDGE_DIM), dtype=jnp.float32)
        W1 = jax.random.normal(ks[4], (EDGE_DIM, MLP_DIM), dtype=jnp.float32) / np.sqrt(EDGE_DIM)
        b1 = jnp.zeros((MLP_DIM,), dtype=jnp.float32)
        W2 = jax.random.normal(ks[5], (MLP_DIM, W_NUMEL), dtype=jnp.float32) / np.sqrt(MLP_DIM)
        b2 = jnp.zeros((W_NUMEL,), dtype=jnp.float32)
        si_w0 = jax.random.normal(ks[6], (MUL, MUL), dtype=jnp.float32)
        si_w1 = jax.random.normal(ks[7], (MUL, MUL), dtype=jnp.float32)
        return {'node_attr': node_attr, 'edge_index': edge_index, 'edge_sh': edge_sh, 'edge_feat': edge_feat, 'W1': W1, 'b1': b1, 'W2': W2, 'b2': b2, 'si_w0': si_w0, 'si_w1': si_w1}
    _L0_gnn_all = _L0_gnn_setup()
    _L0_gnn_in = {k: v for k, v in _L0_gnn_all.items() if k in ('W1', 'b1', 'W2', 'b2', 'si_w0', 'si_w1')}
    del _L0_gnn_all

    def _L1_gnn_setup():
        import jax, jax.numpy as jnp
        import numpy as np
        N = 3125
        E = 50000
        IN_C, HID, OUT_C = (32, 64, 32)

        def _mean_aggregate(x, src, dst, num_nodes):
            summed = jax.ops.segment_sum(x[src], dst, num_segments=num_nodes)
            deg = jax.ops.segment_sum(jnp.ones((src.shape[0],), x.dtype), dst, num_segments=num_nodes)
            return summed / jnp.maximum(deg, 1.0)[:, None]

        def _sage_conv(x, src, dst, W_l, b, W_r):
            agg = _mean_aggregate(x, src, dst, x.shape[0])
            return agg @ W_l + b + x @ W_r
        key = jax.random.key(seed)
        ks = jax.random.split(key, 8)
        x = jax.random.normal(ks[0], (N, IN_C), dtype=jnp.float32)
        edge_index = jax.random.randint(ks[1], (2, E), 0, N, dtype=jnp.int64)
        s1 = 1.0 / np.sqrt(IN_C)
        s2 = 1.0 / np.sqrt(HID)
        W1_l = jax.random.uniform(ks[2], (IN_C, HID), jnp.float32, -s1, s1)
        b1 = jnp.zeros((HID,), jnp.float32)
        W1_r = jax.random.uniform(ks[3], (IN_C, HID), jnp.float32, -s1, s1)
        W2_l = jax.random.uniform(ks[4], (HID, OUT_C), jnp.float32, -s2, s2)
        b2 = jnp.zeros((OUT_C,), jnp.float32)
        W2_r = jax.random.uniform(ks[5], (HID, OUT_C), jnp.float32, -s2, s2)
        return {'x': x, 'edge_index': edge_index, 'W1_l': W1_l, 'b1': b1, 'W1_r': W1_r, 'W2_l': W2_l, 'b2': b2, 'W2_r': W2_r}
    _L1_gnn_all = _L1_gnn_setup()
    _L1_gnn_in = {k: v for k, v in _L1_gnn_all.items() if k in ('W1_l', 'b1', 'W1_r', 'W2_l', 'b2', 'W2_r')}
    del _L1_gnn_all
    return {'x': x, 'src': src, 'dst': dst, 'edge_attr_32': edge_attr_32, 'edge_attr_4': edge_attr_4, 'L0_gnn_W1': _L0_gnn_in['W1'], 'L0_gnn_b1': _L0_gnn_in['b1'], 'L0_gnn_W2': _L0_gnn_in['W2'], 'L0_gnn_b2': _L0_gnn_in['b2'], 'L0_gnn_si_w0': _L0_gnn_in['si_w0'], 'L0_gnn_si_w1': _L0_gnn_in['si_w1'], 'L1_gnn_W1_l': _L1_gnn_in['W1_l'], 'L1_gnn_b1': _L1_gnn_in['b1'], 'L1_gnn_W1_r': _L1_gnn_in['W1_r'], 'L1_gnn_W2_l': _L1_gnn_in['W2_l'], 'L1_gnn_b2': _L1_gnn_in['b2'], 'L1_gnn_W2_r': _L1_gnn_in['W2_r']}

def reference(x, src, dst, edge_attr_32, edge_attr_4, L0_gnn_W1, L0_gnn_b1, L0_gnn_W2, L0_gnn_b2, L0_gnn_si_w0, L0_gnn_si_w1, L1_gnn_W1_l, L1_gnn_b1, L1_gnn_W1_r, L1_gnn_W2_l, L1_gnn_b2, L1_gnn_W2_r):
    import jax
    import jax.numpy as jnp

    def _L0_gnn_ref(node_attr, edge_index, edge_sh, edge_feat, W1, b1, W2, b2, si_w0, si_w1):
        import jax, jax.numpy as jnp
        import numpy as np
        MUL = 8
        N_NODES = 3125
        N_EDGES = 25000
        EDGE_DIM = 32
        MLP_DIM = 64
        W_NUMEL = 4 * MUL * MUL
        ALPHA = 0.25
        C110 = 1.0 / np.sqrt(3.0)
        SI_SCALE = 1.0 / np.sqrt(MUL)
        n = node_attr.shape[0]
        e = edge_sh.shape[0]
        h = jax.nn.relu(edge_feat @ W1 + b1)
        w = (h @ W2 + b2).reshape(e, 4, MUL, MUL)
        w_000, w_011, w_101, w_110 = (w[:, 0], w[:, 1], w[:, 2], w[:, 3])
        s = node_attr[:, :MUL]
        v = node_attr[:, MUL:].reshape(n, MUL, 3)
        src, dst = (edge_index[0], edge_index[1])
        s_e = s[src]
        v_e = v[src]
        sh0 = edge_sh[:, 0]
        sh1 = edge_sh[:, 1:4]
        m0 = ALPHA * (jnp.einsum('ei,eio->eo', s_e * sh0[:, None], w_000) + C110 * jnp.einsum('eim,em,eio->eo', v_e, sh1, w_110))
        m1 = ALPHA * (jnp.einsum('ei,em,eio->eom', s_e, sh1, w_011) + jnp.einsum('eim,eio->eom', v_e * sh0[:, None, None], w_101))
        out0 = jax.ops.segment_sum(m0, dst, num_segments=n)
        out1 = jax.ops.segment_sum(m1.reshape(e, MUL * 3), dst, num_segments=n).reshape(n, MUL, 3)
        out0 = out0 + SI_SCALE * (s @ si_w0)
        out1 = out1 + SI_SCALE * jnp.einsum('nim,io->nom', v, si_w1)
        return jnp.concatenate([out0, out1.reshape(n, MUL * 3)], axis=-1)

    def _L1_gnn_ref(x, edge_index, W1_l, b1, W1_r, W2_l, b2, W2_r):
        import jax, jax.numpy as jnp
        import numpy as np
        N = 3125
        E = 50000
        IN_C, HID, OUT_C = (32, 64, 32)

        def _mean_aggregate(x, src, dst, num_nodes):
            summed = jax.ops.segment_sum(x[src], dst, num_segments=num_nodes)
            deg = jax.ops.segment_sum(jnp.ones((src.shape[0],), x.dtype), dst, num_segments=num_nodes)
            return summed / jnp.maximum(deg, 1.0)[:, None]

        def _sage_conv(x, src, dst, W_l, b, W_r):
            agg = _mean_aggregate(x, src, dst, x.shape[0])
            return agg @ W_l + b + x @ W_r
        src, dst = (edge_index[0], edge_index[1])
        h = jax.nn.relu(_sage_conv(x, src, dst, W1_l, b1, W1_r))
        return _sage_conv(h, src, dst, W2_l, b2, W2_r)
    edge_index = jnp.stack([src, dst])
    h = jnp.maximum(_layernorm(x, axis=-1), 0.0)
    x = x + _L0_gnn_ref(h, edge_index, edge_attr_4, edge_attr_32, L0_gnn_W1, L0_gnn_b1, L0_gnn_W2, L0_gnn_b2, L0_gnn_si_w0, L0_gnn_si_w1)
    h = jnp.maximum(_layernorm(x, axis=-1), 0.0)
    x = x + _L1_gnn_ref(h, edge_index, L1_gnn_W1_l, L1_gnn_b1, L1_gnn_W1_r, L1_gnn_W2_l, L1_gnn_b2, L1_gnn_W2_r)
    return x

_drawn_inputs = setup_inputs


def setup_inputs(seed=0):
    import zlib

    import numpy as np

    out = dict(_drawn_inputs(seed))
    spreads = {'L0_gnn_b1': (0.0, 0.1),
     'L0_gnn_b2': (0.0, 0.1),
     'L1_gnn_b1': (0.0, 0.542),
     'L1_gnn_b2': (0.0, 0.1)}
    factors = {}
    for name, (base, spread) in spreads.items():
        noise = np.random.default_rng([zlib.crc32(name.encode()), seed]).standard_normal(out[name].shape)
        drawn = base * np.exp(spread * noise) if base else spread * noise
        out[name] = jnp.asarray(drawn.astype(out[name].dtype))
    for name, factor in factors.items():
        out[name] = (out[name] * factor).astype(out[name].dtype)
    return out
```

```python
from contextlib import ExitStack

import numpy as np

import concourse.bass as bass
from concourse import mybir
from concourse.alu_op_type import AluOpType as ALU

F32 = mybir.dt.float32
I32 = mybir.dt.int32
U32 = mybir.dt.uint32
ACT = mybir.ActivationFunctionType
AX_X = mybir.AxisListType.X

NODES, EDGES, FEAT = 3125, 53125, 32
MUL = 8
HID0, HID1 = 64, 64
WCOLS = 4 * MUL * MUL
ALPHA, C110, SI_SCALE, EPS = 0.25, 1.0 / np.sqrt(3.0), 1.0 / np.sqrt(8.0), 1e-5

TILE = 125
BLOCKS = NODES // TILE
TILES = EDGES // TILE
GROUP = 5
GROUPS = TILES // GROUP
GEDGES = GROUP * TILE
WINDOW = 64
SHIFT = 6
BODY = 2
BODIES = GROUPS // BODY
USES = [(GROUPS + 1) // 2, GROUPS // 2]
assert BLOCKS * TILE == NODES and TILES * TILE == EDGES and GROUPS * GROUP == TILES
assert GROUPS == BODIES * BODY + 1 and WINDOW == 1 << SHIFT

UNITS = 6
SUMS = UNITS * MUL
SH_SUMS = SUMS + 3 * MUL
DEG = 96
ACC = NODES + WINDOW
CHUNK = 500
BANK = 512


def constants():
    ident = np.eye(128, dtype=np.float32)
    iota = np.tile(np.arange(WINDOW, dtype=np.float32), (128, 1))
    fold = np.zeros((128, FEAT), np.float32)
    for o in range(MUL):
        fold[o, o] = fold[MUL + o, o] = ALPHA
        for m in range(3):
            fold[(2 + m) * MUL + o, MUL + 3 * o + m] = ALPHA
            fold[SUMS + m * MUL + o, MUL + 3 * o + m] = ALPHA
    return np.concatenate([ident, iota, fold], axis=1)


def gnn(nc, x_in, src_in, dst_tiles_in, dst_groups_in, ef_t_in, sh_in, w1_in, b1_in, w2_in, si0_in, si1_in,
        sage1_in, sage1_b_in, sage2_in, sage2_b_in, const_in, out):
    ctx = ExitStack()
    with ctx:
        def sb(name, shape, dt=F32):
            return ctx.enter_context(nc.sbuf_tensor(name, shape, dt))

        def sem(name):
            return ctx.enter_context(nc.semaphore(name))

        tables = [nc.dram_tensor(f"table{ph}", (NODES, FEAT), F32, kind="Internal").ap() for ph in range(3)]

        const = sb("const", [128, 128 + WINDOW + FEAT])
        ident, iota, fold = const[:, 0:128], const[:, 128:128 + WINDOW], const[:, 128 + WINDOW:]
        ones = sb("ones", [128, 128])
        eps = sb("eps", [128, 1])
        w1 = sb("w1", [FEAT, HID0])
        b1 = sb("b1", [HID0, 1])
        w2 = sb("w2", [HID0 + 1, WCOLS])
        si = sb("si", [FEAT, FEAT])
        sage1 = sb("sage1", [2 * FEAT, HID1])
        sage1_b = sb("sage1_b", [HID1, 1])
        sage2 = sb("sage2", [HID1, 2 * FEAT])
        sage2_b = sb("sage2_b", [TILE, FEAT])
        src_all = sb("src_all", [TILE, TILES], U32)
        src_slot = [sb(f"src_slot{s}", [TILE, GROUP], U32) for s in range(2)]
        dst_raw = sb("dst_raw", [TILE, TILES], I32)
        dst_f = sb("dst_f", [TILE, TILES])
        dst_rel = sb("dst_rel", [TILE, TILES])
        dstg_raw = sb("dstg_raw", [GROUPS, GEDGES], I32)
        dstg_f = sb("dstg_f", [GROUPS, GEDGES])
        low_high = sb("low_high", [GROUPS, 3])
        diag = sb("diag", [GROUPS, 2, GROUPS])
        base0 = sb("base0", [128, 2, GROUPS])
        base = sb("base", [128, GROUPS])
        base_row = sb("base_row", [1, GROUPS], I32)
        span_f = sb("span_f", [1, 1])
        span_i = sb("span_i", [1, 1], I32)
        sh_all = sb("sh_all", [TILE, TILES, 4])
        shc_all = sb("shc_all", [TILE, TILES, 3])
        x = sb("x", [TILE, BLOCKS, FEAT])
        xc = sb("xc", [TILE, BLOCKS, FEAT])
        sq = sb("sq", [TILE, BLOCKS, FEAT])
        h = sb("h", [TILE, BLOCKS, FEAT])
        stat = sb("stat", [TILE, 4, BLOCKS])
        acc = sb("acc", [128, ACC])
        h_t = sb("h_t", [FEAT, NODES])
        stack = sb("stack", [2 * FEAT, ACC])
        inv_deg = sb("inv_deg", [FEAT, NODES])
        deg1 = sb("deg1", [FEAT, NODES])
        h1_t = sb("h1_t", [HID1, NODES])
        gath = [sb(f"gath{s}", [TILE, GROUP, FEAT]) for s in range(2)]
        ef = [sb(f"ef{s}", [FEAT, GEDGES]) for s in range(2)]
        hid = [sb(f"hid{s}", [HID0 + 1, GEDGES]) for s in range(2)]
        dprod = sb("dprod", [TILE, GROUP, 3, MUL])
        z_ad = sb("z_ad", [TILE, GROUP, 2, MUL])
        z_v = sb("z_v", [TILE, GROUP, 3 * MUL])
        prod = sb("prod", [TILE, GROUP, UNITS, MUL, MUL])
        msg = [sb(f"msg{s}", [TILE, GROUP, 128]) for s in range(2)]
        hot = [sb(f"hot{s}", [TILE, GROUP, WINDOW]) for s in range(2)]

        psum = ctx.enter_context(nc.psum_tensor("psum", [128, 8, BANK], F32))
        weights_ps = [psum[:TILE, 3 * s:3 * s + 3, :].rearrange("p k n -> p (k n)")[:, 0:GROUP * WCOLS]
                      .rearrange("p (t n) -> p t n", t=GROUP) for s in range(2)]
        FIRST = (GROUP - 1) * TILE
        hid_ps = [[(0, FIRST, psum[:HID0, 6, 0:FIRST]),
                   (FIRST, GEDGES, psum[:HID0, 3 * s + 2, BANK - TILE:BANK])] for s in range(2)]
        window_ps = [[psum[:, 7, 0:WINDOW]] * 2] + [[psum[:FEAT, s, 0:WINDOW] for s in range(2)]] * 2

        const_in_s = sem("const_in_s")
        graph_in = sem("graph_in")
        x_in_s = sem("x_in_s")
        par_in = sem("par_in")
        filled = sem("filled")
        si_zeroed = sem("si_zeroed")
        span_ready = sem("span_ready")
        diag_ready = sem("diag_ready")
        diag_summed = sem("diag_summed")
        var_ready = [sem(f"var_ready{k}") for k in range(2)]
        std_ready = [sem(f"std_ready{k}") for k in range(2)]
        h_ready = [sem(f"h_ready{k}") for k in range(2)]
        table_in = [sem(f"table_in{ph}") for ph in range(3)]
        h_turned = [sem(f"h_turned{k}") for k in range(2)]
        h_t_ready = [sem(f"h_t_ready{k}") for k in range(2)]
        out0_summed = sem("out0_summed")
        mean_ready = [sem(f"mean_ready{k}") for k in range(2)]
        sage1_summed = sem("sage1_summed")
        h1_ready = sem("h1_ready")
        y_summed = sem("y_summed")
        y_ready = sem("y_ready")
        agg_turned = sem("agg_turned")
        out_ready = sem("out_ready")
        out_stored = sem("out_stored")
        step_dve = sem("step_dve")
        src_copied = [sem(f"src_copied{ph}") for ph in range(3)]
        gathered = [[sem(f"gathered{ph}{s}") for s in range(2)] for ph in range(3)]
        gath_read = sem("gath_read")
        hot_ready = [sem(f"hot_ready{ph}") for ph in range(3)]
        summed = [sem(f"summed{ph}") for ph in range(3)]
        added = [sem(f"added{ph}") for ph in range(3)]
        base_ready = [sem(f"base_ready{ph}") for ph in range(3)]
        ef_in = [sem(f"ef_in{s}") for s in range(2)]
        hid_summed = sem("hid_summed")
        hid_ready = sem("hid_ready")
        weights_ready = sem("weights_ready")
        weights_read = sem("weights_read")
        link = sem("link")
        msg_ready = sem("msg_ready")

        PARS = 0

        def passes(eng):
            eng.wait_ge(span_ready, 1)
            span = eng.value_load(span_i[0:1, 0:1], min_val=0, max_val=NODES - 1)
            return eng.snap((span >> SHIFT) + 1, min_val=1, max_val=(NODES - 1) // WINDOW + 1)

        def over_groups(eng, n_pass, step, finish):
            with eng.Fori(0, n_pass) as j:
                n0 = eng.snap(j * GROUPS)
                u = [eng.snap(j * USES[s]) for s in range(2)]
                for s in range(2):
                    step(s, n0 + s, s, u[s], True)
                with eng.Fori(1, BODIES) as b:
                    g = eng.snap(b * 2)
                    n = eng.snap(n0 + g)
                    for s in range(2):
                        step(g + s, n + s, s, u[s] + b, False)
                step(GROUPS - 1, n0 + (GROUPS - 1), 0, u[0] + BODIES, False)
                finish(j)

        def of_block(t, b):
            return t[:, b:b + (TILE - 1) * BLOCKS + 1:BLOCKS]

        block = ctx.enter_context(nc.Block())

        @block.sync
        def _(sp):
            sp.dma_start(const[:, :], const_in).then_inc(const_in_s, 16)
            sp.dma_start(dstg_raw[:, :], dst_groups_in).then_inc(graph_in, 16)
            sp.dma_start(x[:, :, :], x_in.rearrange("(p b) f -> p b f", b=BLOCKS)).then_inc(x_in_s, 16)
            sp.dma_start(dst_raw[:, :], dst_tiles_in).then_inc(graph_in, 16)
            sp.dma_start(src_all[:, :], src_in.bitcast(U32)).then_inc(graph_in, 16)
            sp.dma_start(sh_all[:, :, :], sh_in).then_inc(graph_in, 16)
            sp.wait_ge(si_zeroed, 1)
            sp.dma_start(si[0:MUL, 0:MUL], si0_in).then_inc(par_in, 16)
            for m in range(3):
                sp.dma_start(si[MUL * (m + 1):MUL * (m + 2), MUL + m:MUL + m + 3 * MUL - 2:3], si1_in,
                             allow_slow_non_contiguous=True).then_inc(par_in, 16)
            n_pass = passes(sp)

            def load_edges(g, n, s, use, first):
                if not first:
                    sp.wait_ge(hid_summed, n - 1)
                sp.dma_start(ef[s][:, :], ef_t_in[:, bass.ds(g * GEDGES, GEDGES)]).then_inc(ef_in[s], 16)

            def next_pass(j):
                sp.wait_ge(added[0], (j + 1) * GROUPS)

            over_groups(sp, n_pass, load_edges, next_pass)
            sp.wait_ge(out_stored, 16)

        @block.gpsimd
        def _(pool):
            nc.gpsimd.memset(si[:, :], 0.0).then_inc(si_zeroed, 1)
            n_pass = passes(pool)
            for ph in range(3):
                def gather(g, n, s, use, first, ph=ph):
                    pool.wait_ge(src_copied[ph], n + 1)
                    if not first:
                        pool.wait_ge(gath_read if ph == 0 else summed[ph], n - 1)
                    pool.wait_ge(table_in[ph], 16)
                    pool.nop(nofuse=True)
                    for t in range(GROUP):
                        pool.indirect_dma_start(
                            out=gath[s][:, t, :], out_offset=None, in_=tables[ph],
                            in_offset=bass.IndirectOffsetOnAxis(ap=src_slot[s][:, t:t + 1], axis=0),
                        ).then_inc(gathered[ph][s], 16)

                def next_pass(j, ph=ph):
                    pool.wait_ge(added[ph], (j + 1) * GROUPS)

                over_groups(pool, n_pass, gather, next_pass)

        @block.scalar
        def _(act):
            act.dma_start(w1[:, :], w1_in).then_inc(par_in, 16)
            act.dma_start(b1[:, :], b1_in).then_inc(par_in, 16)
            act.dma_start(w2[:, :], w2_in).then_inc(par_in, 16)
            act.dma_start(sage1[:, :], sage1_in).then_inc(par_in, 16)
            act.dma_start(sage1_b[:, :], sage1_b_in).then_inc(par_in, 16)
            act.dma_start(sage2[:, :], sage2_in).then_inc(par_in, 16)
            act.dma_start(sage2_b[:, :], sage2_b_in.broadcast_to([TILE, FEAT])).then_inc(par_in, 16)
            act.wait_ge(filled, 1)

            def std_and_table(k):
                act.wait_ge(var_ready[k], 1)
                nc.scalar.activation(stat[:, 2, :], stat[:, 1, :], ACT.Sqrt, bias=eps[:TILE, :],
                                     scale=1.0 / FEAT).then_inc(std_ready[k], 1)
                act.wait_ge(h_ready[k], 1)
                act.dma_start(tables[k].rearrange("(p b) f -> p b f", b=BLOCKS), h[:, :, :]).then_inc(table_in[k], 16)
                act.wait_ge(h_turned[k], 1)
                to = h_t[:, :] if k == 0 else stack[FEAT:2 * FEAT, 0:NODES]
                to = to.rearrange("f (p b) -> f b p", b=BLOCKS)
                for c in range(0, BLOCKS, 4):
                    w = min(4, BLOCKS - c)
                    last = nc.scalar.copy(to[:, c:c + w, :],
                                          psum[:FEAT, c // 4, 0:w * TILE].rearrange("f (b p) -> f b p", b=w))
                last.then_inc(h_t_ready[k], 1)

            std_and_table(0)
            n_pass = passes(act)
            act.wait_ge(par_in, 16 * 11)
            act.wait_ge(graph_in, 64)
            for ph in range(3):
                def copy_src_and_relu(g, n, s, use, first, ph=ph):
                    if not first:
                        act.wait_ge(gathered[ph][s], use * (16 * GROUP))
                    nc.scalar.copy(src_slot[s][:, :], src_all[:, bass.ds(g * GROUP, GROUP)]).then_inc(src_copied[ph], 1)
                    if ph == 0:
                        act.wait_ge(hid_summed, n + 1)
                        if not first:
                            act.wait_ge(weights_ready, n - 1)
                        for a, z, ps in hid_ps[s]:
                            last = nc.scalar.activation(hid[s][0:HID0, a:z], ps, ACT.Relu,
                                                        bias=b1[:, 0:1])
                        last.then_inc(hid_ready, 1)

                def next_pass(j, ph=ph):
                    act.wait_ge(added[ph], (j + 1) * GROUPS)

                over_groups(act, n_pass, copy_src_and_relu, next_pass)
                if ph == 0:
                    std_and_table(1)
                elif ph == 1:
                    act.wait_ge(sage1_summed, 1)
                    for k, a in enumerate(range(0, NODES, CHUNK)):
                        w = min(CHUNK, NODES - a)
                        last = nc.scalar.activation(h1_t[:, a:a + w], psum[:HID1, k, 0:w], ACT.Relu,
                                                    bias=sage1_b[:, 0:1])
                    last.then_inc(h1_ready, 1)
                    act.wait_ge(y_ready, 1)
                    act.dma_start(tables[2].rearrange("(p b) f -> p b f", b=BLOCKS), h[:, :, :]).then_inc(table_in[2], 16)
            act.wait_ge(out_ready, 1)
            act.dma_start(out.rearrange("(p b) f -> p b f", b=BLOCKS), h[:, :, :]).then_inc(out_stored, 16)

        @block.tensor
        def _(pe):
            pe.wait_ge(diag_ready, 1)
            nc.tensor.matmul(psum[:, 7, 0:2 * GROUPS], ones[0:GROUPS, :], diag[:, :, :], start=True,
                             stop=True).then_inc(diag_summed, 1)

            def turn_h(k):
                pe.wait_ge(h_ready[k], 1)
                for b in range(BLOCKS):
                    last = nc.tensor.transpose(psum[:FEAT, b // 4, (b % 4) * TILE:(b % 4 + 1) * TILE], h[:, b, :],
                                               ident[:TILE, :TILE])
                last.then_inc(h_turned[k], 1)

            turn_h(0)
            n_pass = passes(pe)
            pe.wait_ge(par_in, 16 * 11)
            pe.wait_ge(filled, 1)
            pe.wait_ge(h_t_ready[0], 1)
            for ph in range(3):
                def hidden(g, n, s, use, first):
                    pe.wait_ge(ef_in[s], (use + 1) * 16)
                    if not (first and s == 0):
                        pe.wait_ge(hid_ready, n)
                    if not first:
                        pe.wait_ge(weights_read, n - 1)
                    for a, z, ps in hid_ps[s]:
                        last = nc.tensor.matmul(ps, w1[:, :], ef[s][:, a:z], start=True, stop=True)
                    last.then_inc(hid_summed, 1)
                    pe.wait_ge(hid_ready, n + 1)
                    for t in range(GROUP):
                        last = nc.tensor.matmul(weights_ps[s][:, t, :], hid[s][:, t * TILE:(t + 1) * TILE], w2[:, :],
                                                start=True, stop=True)
                    last.then_inc(weights_ready, 1)

                def window(g, n, s, use, first, ph=ph):
                    rows = msg[s] if ph == 0 else gath[s]
                    width = 128 if ph == 0 else FEAT
                    if ph == 0:
                        pe.wait_ge(msg_ready, n + 1)
                    else:
                        pe.wait_ge(gathered[ph][s], (use + 1) * (16 * GROUP))
                        pe.wait_ge(hot_ready[ph], n + 1)
                    if ph == 0 and not (first and s == 0):
                        pe.wait_ge(added[ph], n)
                    elif ph and not first:
                        pe.wait_ge(added[ph], n - 1)
                    for t in range(GROUP):
                        last = nc.tensor.matmul(window_ps[ph][s][:width, :], rows[:, t, :], hot[s][:, t, :], start=(t == 0),
                                                stop=(t == GROUP - 1))
                    last.then_inc(summed[ph], 1)

                if ph == 0:
                    with pe.Fori(0, n_pass) as j:
                        n0 = pe.snap(j * GROUPS)
                        u = [pe.snap(j * USES[s]) for s in range(2)]
                        hidden(0, n0, 0, u[0], True)
                        hidden(1, n0 + 1, 1, u[1], True)
                        window(0, n0, 0, u[0], True)
                        with pe.Fori(1, BODIES) as b:
                            n = pe.snap(n0 + b * 2)
                            hidden(None, n, 0, u[0] + b, False)
                            if True:
                                window(None, n - 1, 1, None, False)
                            hidden(None, n + 1, 1, u[1] + b, False)
                            window(None, n, 0, None, False)
                        hidden(GROUPS - 1, n0 + (GROUPS - 1), 0, u[0] + BODIES, False)
                        window(None, n0 + (GROUPS - 2), 1, None, False)
                        window(None, n0 + (GROUPS - 1), 0, None, False)
                        pe.wait_ge(added[0], (j + 1) * GROUPS)
                    for b in range(BLOCKS):
                        to = psum[:TILE, b // 16, (b % 16) * FEAT:(b % 16 + 1) * FEAT]
                        nc.tensor.matmul(to, of_block(acc, b), fold, start=True, stop=False)
                        last = nc.tensor.matmul(to, of_block(h_t, b), si[:, :], start=False, stop=True)
                    last.then_inc(out0_summed, 1)
                    turn_h(1)
                    pe.wait_ge(h_t_ready[1], 1)
                else:
                    def next_pass(j, ph=ph):
                        pe.wait_ge(added[ph], (j + 1) * GROUPS)

                    over_groups(pe, n_pass, window, next_pass)
                    pe.wait_ge(mean_ready[ph - 1], 1)
                    if ph == 1:
                        for k, a in enumerate(range(0, NODES, CHUNK)):
                            w = min(CHUNK, NODES - a)
                            last = nc.tensor.matmul(psum[:HID1, k, 0:w], sage1[:, :], stack[:, a:a + w], start=True,
                                                    stop=True)
                        last.then_inc(sage1_summed, 1)
                        pe.wait_ge(h1_ready, 1)
                        for b in range(BLOCKS):
                            last = nc.tensor.matmul(psum[:TILE, b // 8, (b % 8) * 2 * FEAT:(b % 8 + 1) * 2 * FEAT],
                                                    of_block(h1_t, b), sage2[:, :], start=True, stop=True)
                        last.then_inc(y_summed, 1)
                        pe.wait_ge(y_ready, 1)
                    else:
                        for b in range(BLOCKS):
                            last = nc.tensor.matmul(psum[:TILE, b // 16, (b % 16) * FEAT:(b % 16 + 1) * FEAT],
                                                    of_block(stack[0:FEAT, :], b), ident[:FEAT, :FEAT], start=True,
                                                    stop=True)
                        last.then_inc(agg_turned, 1)

        @block.vector
        def _(dve):
            vec = nc.vector
            steps = [0]

            def done(ins):
                steps[0] += 1
                ins.then_inc(step_dve, 1)
                dve.wait_ge(step_dve, steps[0])

            vec.memset(eps[:, :], EPS)
            vec.memset(ones[:, :], 1.0)
            vec.memset(acc[:, :], 0.0)
            for s in range(2):
                vec.memset(msg[s][:, :, SH_SUMS:DEG], 0.0)
                vec.memset(msg[s][:, :, DEG:128], 1.0)
                last = vec.memset(hid[s][HID0:HID0 + 1, :], 1.0)
            last.then_inc(filled, 1)

            dve.wait_ge(const_in_s, 16)
            dve.wait_ge(graph_in, 64)
            done(vec.tensor_copy(dstg_f[:, :], dstg_raw[:, :]))
            vec.tensor_reduce(low_high[:, 0:1], dstg_f[:, :], AX_X, ALU.min)
            done(vec.tensor_reduce(low_high[:, 1:2], dstg_f[:, :], AX_X, ALU.max))
            done(vec.tensor_tensor(low_high[:, 2:3], low_high[:, 1:2], low_high[:, 0:1], ALU.subtract))
            vec.tensor_scalar(diag[:, 0, :], ident[:GROUPS, :GROUPS], low_high[:, 0:1], None, ALU.mult)
            vec.tensor_scalar(diag[:, 1, :], ident[:GROUPS, :GROUPS], low_high[:, 2:3], None,
                              ALU.mult).then_inc(diag_ready, 1)
            dve.wait_ge(diag_summed, 1)
            done(vec.tensor_copy(base0[:, :, :], psum[:, 7, 0:2 * GROUPS].rearrange("p (k g) -> p k g", k=2)))
            done(vec.tensor_reduce(span_f[:, :], base0[0:1, 1, :], AX_X, ALU.max))
            vec.tensor_copy(span_i[:, :], span_f[:, :]).then_inc(span_ready, 1)
            vec.tensor_copy(dst_f[:, :], dst_raw[:, :])
            vec.tensor_scalar(shc_all[:, :, :], sh_all[:, :, 1:4], float(C110), None, ALU.mult)
            dve.wait_ge(par_in, 16 * 11)
            done(vec.tensor_scalar(si[:, :], si[:, :], float(SI_SCALE), None, ALU.mult))

            def layernorm_relu(k):
                done(vec.tensor_reduce(stat[:, 0, :], x[:, :, :], AX_X, ALU.add))
                done(vec.tensor_scalar(stat[:, 0, :], stat[:, 0, :], 1.0 / FEAT, None, ALU.mult))
                done(vec.tensor_tensor(xc[:, :, :], x[:, :, :], stat[:, 0, :].broadcast_to_dim(FEAT)
                                       if False else spread(stat[:, 0, :], FEAT), ALU.subtract))
                done(vec.tensor_tensor(sq[:, :, :], xc[:, :, :], xc[:, :, :], ALU.mult))
                vec.tensor_reduce(stat[:, 1, :], sq[:, :, :], AX_X, ALU.add).then_inc(var_ready[k], 1)
                dve.wait_ge(std_ready[k], 1)
                done(vec.reciprocal(stat[:, 3, :], stat[:, 2, :]))
                done(vec.tensor_tensor(xc[:, :, :], xc[:, :, :], spread(stat[:, 3, :], FEAT), ALU.mult))
                if k == 0:
                    vec.tensor_scalar(h[:, :, 0:MUL], xc[:, :, 0:MUL], 0.0, None, ALU.max)
                    vec.tensor_scalar(h[:, :, MUL:FEAT].rearrange("p b (m i) -> p b m i", m=3),
                                      xc[:, :, MUL:FEAT].rearrange("p b (i m) -> p b m i", m=3), 0.0, None,
                                      ALU.max).then_inc(h_ready[k], 1)
                else:
                    vec.tensor_scalar(h[:, :, :], xc[:, :, :], 0.0, None, ALU.max).then_inc(h_ready[k], 1)

            def spread(a, n):
                return a.unsqueeze(2).to_broadcast([a.shape[0], a.shape[1], n])

            dve.wait_ge(x_in_s, 16)
            layernorm_relu(0)
            n_pass = passes(dve)

            def place_windows(ph, j, sums):
                vec.tensor_tensor(dst_rel[:, :].rearrange("p (g t) -> p g t", t=GROUP),
                                  dst_f[:, :].rearrange("p (g t) -> p g t", t=GROUP), spread(base[:TILE, :], GROUP),
                                  ALU.subtract)
                vec.tensor_copy(base_row[:, :], base[0:1, :]).then_inc(base_ready[ph], 1)
                dve.wait_ge(base_ready[ph], j * 2 + 1)

            def move_windows(ph, j):
                dve.wait_ge(added[ph], (j + 1) * GROUPS)
                vec.tensor_scalar(base[:, :], base[:, :], float(WINDOW), float(NODES), ALU.add,
                                  ALU.min).then_inc(base_ready[ph], 1)
                dve.wait_ge(base_ready[ph], j * 2 + 2)

            def one_hot(g, s):
                rel = dst_rel[:, bass.ds(g * GROUP, GROUP)]
                return vec.tensor_tensor(hot[s][:, :, :],
                                         iota[:TILE, :].unsqueeze(1).to_broadcast([TILE, GROUP, WINDOW]),
                                         spread(rel, WINDOW), ALU.is_equal)

            def add_window(ph, g, n, s, sums, first=False):
                at = dve.value_load(base_row[0:1, bass.ds(g, 1)], min_val=0, max_val=NODES)
                dve.wait_ge(summed[ph], n + 1)
                if not first:
                    dve.wait_ge(added[ph], n)
                to = sums[:, bass.ds(at, WINDOW)]
                vec.tensor_tensor(to, to, window_ps[ph][s], ALU.add).then_inc(added[ph], 1)

            LINKS = 4

            def messages(g, n, s, use, first, add_before=None):
                sh = sh_all[:, bass.ds(g * GROUP, GROUP), :]
                shc = shc_all[:, bass.ds(g * GROUP, GROUP), :]
                c = dve.snap(n * LINKS)
                rows = gath[s]
                dve.wait_ge(gathered[0][s], (use + 1) * (16 * GROUP))
                vec.tensor_tensor(dprod[:, :, :, :], rows[:, :, MUL:FEAT].rearrange("p t (m i) -> p t m i", m=3),
                                  shc.unsqueeze(3).to_broadcast([TILE, GROUP, 3, MUL]), ALU.mult).then_inc(link, 1)
                sh0 = sh[:, :, 0:1]
                vec.tensor_tensor(z_v[:, :, :], rows[:, :, MUL:FEAT], sh0.to_broadcast([TILE, GROUP, 3 * MUL]),
                                  ALU.mult)
                vec.tensor_tensor(z_ad[:, :, 0, :], rows[:, :, 0:MUL], sh0.to_broadcast([TILE, GROUP, MUL]), ALU.mult)
                dve.wait_ge(link, c + 1)
                vec.tensor_reduce(z_ad[:, :, 1, :], dprod[:, :, :, :].rearrange("p t m i -> p t i m"), AX_X,
                                  ALU.add).then_inc(link, 1)
                dve.wait_ge(weights_ready, n + 1)
                w = weights_ps[s]
                vec.tensor_tensor(prod[:, :, 5, :, :], w[:, :, 192:256].rearrange("p t (i o) -> p t i o", i=MUL),
                                  rows[:, :, 0:MUL].unsqueeze(3).to_broadcast([TILE, GROUP, MUL, MUL]),
                                  ALU.mult).then_inc(gath_read, 1)
                dve.wait_ge(link, c + 2)
                vec.tensor_tensor(
                    prod[:, :, 2:5, :, :].rearrange("p t m i o -> p t (m i) o"),
                    w[:, :, 128:192].rearrange("p t (m n) -> p t m n", m=1).to_broadcast([TILE, GROUP, 3, 64]),
                    z_v[:, :, :].unsqueeze(3).to_broadcast([TILE, GROUP, 3 * MUL, MUL]), ALU.mult)
                vec.tensor_tensor(prod[:, :, 0:2, :, :].rearrange("p t c i o -> p t (c i) o"),
                                  w[:, :, 0:128].rearrange("p t (i o) -> p t i o", o=MUL),
                                  z_ad[:, :, :, :].rearrange("p t c i -> p t (c i)").unsqueeze(3)
                                  .to_broadcast([TILE, GROUP, 2 * MUL, MUL]), ALU.mult).then_inc(weights_read, 1)
                if not first:
                    dve.wait_ge(summed[0], n - 1)
                one_hot(g, s).then_inc(link, 1)
                if add_before is not None:
                    add_window(0, add_before, n - 1, 1 - s, acc, first=first)
                dve.wait_ge(weights_read, n + 1)
                for t0, t1 in ((0, 1),):
                    vec.tensor_reduce(msg[s][:, :, 0:SUMS].rearrange("p t (c o) -> p t c o", c=UNITS),
                                      prod[:, :, :, :, :].rearrange("p t c i o -> p t c o i"), AX_X,
                                      ALU.add).then_inc(link, 1)
                dve.wait_ge(link, c + 4)
                vec.tensor_tensor(msg[s][:, :, SUMS:SH_SUMS].rearrange("p t (m o) -> p t m o", m=3),
                                  msg[s][:, :, SUMS - MUL:SUMS].unsqueeze(2).to_broadcast([TILE, GROUP, 3, MUL]),
                                  sh[:, :, 1:4].unsqueeze(3).to_broadcast([TILE, GROUP, 3, MUL]),
                                  ALU.mult).then_inc(msg_ready, 1)
                vec.nop().then_inc(link, 1) if False else None

            for ph in range(3):
                sums = acc if ph == 0 else stack[0:FEAT, :]
                if ph:
                    vec.memset(sums[:, :], 0.0)
                done(vec.tensor_copy(base[:, :], base0[:, 0, :]))
                if ph == 0:
                    with dve.Fori(0, n_pass) as j:
                        n0 = dve.snap(j * GROUPS)
                        u = [dve.snap(j * USES[s]) for s in range(2)]
                        place_windows(0, j, sums)
                        messages(0, n0, 0, u[0], True)
                        messages(1, n0 + 1, 1, u[1], True, 0)
                        with dve.Fori(1, BODIES) as b:
                            g = dve.snap(b * 2)
                            n = dve.snap(n0 + g)
                            messages(g, n, 0, u[0] + b, False, g - 1)
                            messages(g + 1, n + 1, 1, u[1] + b, False, g)
                        messages(GROUPS - 1, n0 + (GROUPS - 1), 0, u[0] + BODIES, False, GROUPS - 2)
                        add_window(0, GROUPS - 1, n0 + (GROUPS - 1), 0, sums)
                        move_windows(0, j)
                    done(vec.tensor_scalar(deg1[:, :], acc[DEG:128, 0:NODES], 1.0, None, ALU.max))
                    vec.reciprocal(inv_deg[:, :], deg1[:, :])
                    dve.wait_ge(out0_summed, 1)
                    for k, (a, z) in enumerate(((0, 16), (16, BLOCKS))):
                        last = vec.tensor_tensor(x[:, a:z, :], x[:, a:z, :],
                                                 psum[:TILE, k, 0:(z - a) * FEAT].rearrange("p (b f) -> p b f", f=FEAT),
                                                 ALU.add)
                    done(last)
                    layernorm_relu(1)
                else:
                    def hot_and_add(g, n, s, use, first, ph=ph, sums=sums):
                        if not first:
                            dve.wait_ge(summed[ph], n - 1)
                        one_hot(g, s).then_inc(hot_ready[ph], 1)
                        add_window(ph, g, n, s, sums, first=first and s == 0)

                    with dve.Fori(0, n_pass) as j:
                        n0 = dve.snap(j * GROUPS)
                        place_windows(ph, j, sums)
                        for s in range(2):
                            hot_and_add(s, n0 + s, s, None, True)
                        with dve.Fori(1, BODIES) as b:
                            g = dve.snap(b * 2)
                            n = dve.snap(n0 + g)
                            for s in range(2):
                                hot_and_add(g + s, n + s, s, None, False)
                        hot_and_add(GROUPS - 1, n0 + (GROUPS - 1), 0, None, False)
                        move_windows(ph, j)
                    vec.tensor_tensor(sums[:, 0:NODES], sums[:, 0:NODES], inv_deg[:, :],
                                      ALU.mult).then_inc(mean_ready[ph - 1], 1)
                    if ph == 1:
                        dve.wait_ge(y_summed, 1)
                        for k, a in enumerate(range(0, BLOCKS, 8)):
                            z = min(a + 8, BLOCKS)
                            y = psum[:TILE, k, 0:(z - a) * 2 * FEAT].rearrange("p (b f) -> p b f", f=2 * FEAT)
                            vec.tensor_copy(h[:, a:z, :], y[:, :, 0:FEAT])
                            last = vec.tensor_tensor(x[:, a:z, :], x[:, a:z, :], y[:, :, FEAT:2 * FEAT], ALU.add)
                        done(last)
                        vec.tensor_tensor(x[:, :, :], x[:, :, :],
                                          sage2_b[:, :].unsqueeze(1).to_broadcast([TILE, BLOCKS, FEAT]),
                                          ALU.add).then_inc(y_ready, 1)
                    else:
                        dve.wait_ge(agg_turned, 1)
                        dve.wait_ge(table_in[2], 16)
                        for k, (a, z) in enumerate(((0, 16), (16, BLOCKS))):
                            last = vec.tensor_tensor(h[:, a:z, :], x[:, a:z, :],
                                                     psum[:TILE, k, 0:(z - a) * FEAT].rearrange(
                                                         "p (b f) -> p b f", f=FEAT), ALU.add)
                        last.then_inc(out_ready, 1)


def kernel(**inputs):
    import concourse.bacc as _bacc
    from concourse.bass_utils import run_bass_kernel_spmd as _run

    a = {k: np.asarray(v) for k, v in inputs.items()}
    order = [0, 3, 2, 1]
    w2 = np.concatenate([a["L0_gnn_W2"], a["L0_gnn_b2"][None]], axis=0).reshape(HID0 + 1, 4, MUL * MUL)[:, order]
    laid = {
        "x": a["x"],
        "src": a["src"].reshape(TILES, TILE).T,
        "dst_tiles": a["dst"].reshape(TILES, TILE).T,
        "dst_groups": a["dst"].reshape(GROUPS, GEDGES),
        "ef_t": a["edge_attr_32"].T,
        "sh": a["edge_attr_4"].reshape(TILES, TILE, 4).transpose(1, 0, 2),
        "w1": a["L0_gnn_W1"], "b1": a["L0_gnn_b1"].reshape(HID0, 1), "w2": w2.reshape(HID0 + 1, WCOLS),
        "si0": a["L0_gnn_si_w0"], "si1": a["L0_gnn_si_w1"],
        "sage1": np.concatenate([a["L1_gnn_W1_l"], a["L1_gnn_W1_r"]], axis=0),
        "sage1_b": a["L1_gnn_b1"].reshape(HID1, 1),
        "sage2": np.concatenate([a["L1_gnn_W2_l"], a["L1_gnn_W2_r"]], axis=1),
        "sage2_b": a["L1_gnn_b2"].reshape(1, FEAT),
        "const": constants(),
    }
    nc = _bacc.Bacc("TRN2", target_bir_lowering=False, num_devices=1)
    arrays, args = {}, []
    for name, v in laid.items():
        v = np.ascontiguousarray(v)
        arrays[f"in_{name}_dram"] = v
        args.append(nc.dram_tensor(f"in_{name}_dram", v.shape, mybir.dt.from_np(v.dtype), kind="ExternalInput").ap())
    args.append(nc.dram_tensor("out_dram", (NODES, FEAT), F32, kind="ExternalOutput").ap())
    gnn(nc, *args)
    r = _run(nc, [arrays], core_ids=[0])
    return r.results[0]["out_dram"]
```

```python
from contextlib import ExitStack

import numpy as np

import concourse.bass as bass
from concourse import mybir
from concourse.alu_op_type import AluOpType as ALU

F32 = mybir.dt.float32
I32 = mybir.dt.int32
I16 = mybir.dt.int16
BF16 = mybir.dt.bfloat16
U32 = mybir.dt.uint32
ACT = mybir.ActivationFunctionType
AX_X = mybir.AxisListType.X

NODES, EDGES, FEAT = 3125, 53125, 32
MUL = 8
HID0, HID1 = 64, 64
WCOLS = 4 * MUL * MUL
ALPHA, C110, SI_SCALE, EPS = 0.25, 1.0 / np.sqrt(3.0), 1.0 / np.sqrt(8.0), 1e-5

TILE = 125
BLOCKS = NODES // TILE
TILES = EDGES // TILE
GROUP = 5
GROUPS = TILES // GROUP
GEDGES = GROUP * TILE
WINDOW = 64
SHIFT = 6
BODY = 2
BODIES = GROUPS // BODY
USES = [(GROUPS + 1) // 2, GROUPS // 2]
UNIT, POOLED = 5, 3
DENSE = UNIT - POOLED
UNITS_OF = GROUPS // UNIT
DEDGES = DENSE * GEDGES
PIECE = UNITS_OF * DEDGES // GROUPS
PARTS = 3
RING = 5
assert UNITS_OF * UNIT == GROUPS and PIECE * GROUPS == UNITS_OF * DEDGES and BLOCKS % RING == 0
assert BLOCKS * TILE == NODES and TILES * TILE == EDGES and GROUPS * GROUP == TILES
assert GROUPS == BODIES * BODY + 1 and WINDOW == 1 << SHIFT

UNITS = 6
SUMS = UNITS * MUL
SH_SUMS = SUMS + 3 * MUL
DEG = 96
ACC = NODES + WINDOW
OUT0 = FEAT + 1
OUT0_BLOCKS = 15
CHUNK = 500
BANK = 512


def constants():
    ident = np.eye(128, dtype=np.float32)
    iota = np.tile(np.arange(WINDOW, dtype=np.float32), (128, 1))
    fold = np.zeros((128, FEAT + 1), np.float32)
    fold[DEG, FEAT] = 1.0
    for o in range(MUL):
        fold[o, o] = fold[5 * MUL + o, o] = ALPHA
        for m in range(3):
            fold[(1 + m) * MUL + o, MUL + 3 * o + m] = ALPHA
            fold[SUMS + m * MUL + o, MUL + 3 * o + m] = ALPHA
    ids = np.zeros((128, BLOCKS), np.float32)
    ids[:TILE] = np.arange(NODES, dtype=np.float32).reshape(TILE, BLOCKS)
    return np.concatenate([ident, iota, fold, ids], axis=1)


def gnn(nc, x_in, src_in, src_dense_in, dst_tiles_in, dst_groups_in, ef_t_in, sh_in, w1_in, b1_in, w2_in, si0_in, si1_in,
        sage1_in, sage1_b_in, sage2_in, sage2_b_in, const_in, out):
    ctx = ExitStack()
    with ctx:
        def sb(name, shape, dt=F32):
            return ctx.enter_context(nc.sbuf_tensor(name, shape, dt))

        def sem(name):
            return ctx.enter_context(nc.semaphore(name))

        tables = [nc.dram_tensor(f"table{ph}", (NODES, FEAT), F32, kind="Internal").ap() for ph in range(3)]

        const = sb("const", [128, 128 + WINDOW + FEAT + 1 + BLOCKS])
        ident, iota = const[:, 0:128], const[:, 128:128 + WINDOW]
        fold, ids = const[:, 128 + WINDOW:129 + WINDOW + FEAT], const[:, 129 + WINDOW + FEAT:]
        ones = sb("ones", [128, 128])
        eps = sb("eps", [128, 1])
        w1 = sb("w1", [128, HID0])
        b1 = sb("b1", [HID0, 1])
        w2 = sb("w2", [128, WCOLS])
        si = sb("si", [FEAT, FEAT])
        sage1 = sb("sage1", [2 * FEAT, HID1])
        sage1_b = sb("sage1_b", [HID1, 1])
        sage2 = sb("sage2", [HID1, 2 * FEAT])
        sage2_b = sb("sage2_b", [TILE, FEAT])
        src_all = sb("src_all", [TILE, TILES], U32)
        src_slot = [sb(f"src_slot{s}", [TILE, GROUP], U32) for s in range(2)]
        dst_raw = sb("dst_raw", [TILE, TILES], I32)
        dst_f = sb("dst_f", [TILE, TILES])
        dst_rel = sb("dst_rel", [TILE, TILES])
        dstg_raw = sb("dstg_raw", [GROUPS, GEDGES], I32)
        dstg_f = sb("dstg_f", [GROUPS, GEDGES])
        low_high = sb("low_high", [GROUPS, 3])
        diag = sb("diag", [GROUPS, 2, GROUPS])
        base0 = sb("base0", [128, 2, GROUPS])
        base = sb("base", [128, GROUPS])
        base_row = sb("base_row", [1, GROUPS], I32)
        span_f = sb("span_f", [1, 1])
        span_i = sb("span_i", [1, 1], I32)
        sh_all = sb("sh_all", [TILE, TILES, 4])
        shc_all = sb("shc_all", [TILE, TILES, 3])
        x = sb("x", [TILE, BLOCKS, FEAT])
        xc = sb("xc", [TILE, BLOCKS, FEAT])
        sq = sb("sq", [TILE, BLOCKS, FEAT])
        h = sb("h", [TILE, BLOCKS, FEAT])
        stat = sb("stat", [TILE, 4, BLOCKS])
        acc = sb("acc", [128, ACC])
        h_t = sb("h_t", [FEAT, NODES])
        stack = sb("stack", [2 * FEAT, ACC])
        degree = sb("degree", [TILE, BLOCKS])
        inv = sb("inv", [TILE, BLOCKS])
        inv_deg = sb("inv_deg", [FEAT, NODES])
        h1_t = acc[0:HID1, 0:NODES]
        gath = [sb(f"gath{s}", [TILE, GROUP, FEAT]) for s in range(2)]
        ef = [sb(f"ef{s}", [128, GEDGES]) for s in range(2)]
        hid = [sb(f"hid{s}", [128, GEDGES]) for s in range(2)]
        dprod = sb("dprod", [TILE, GROUP, 3, MUL])
        z_av = [sb(f"z_av{s}", [TILE, GROUP, FEAT]) for s in range(2)]
        z_sd = [sb(f"z_sd{s}", [TILE, GROUP, 2, MUL]) for s in range(2)]
        distance = [sb(f"distance{s}", [TILE, GROUP, WINDOW]) for s in range(2)]
        prod = sb("prod", [TILE, GROUP, UNITS, MUL, MUL])
        msg = [sb(f"msg{s}", [TILE, GROUP, 128]) for s in range(2)]
        hot = [sb(f"hot{s}", [TILE, GROUP, WINDOW]) for s in range(2)]

        src_raw = [sb(f"src_raw{s}", [128, PIECE], I32) for s in range(2)]
        src16 = sb("src16", [128, UNITS_OF * DEDGES], I16)
        pool_src = [sb(f"pool_src{q}", [TILE, GROUP], U32) for q in range(POOLED)]
        pool_rows = [sb(f"pool_rows{q}", [TILE, GROUP, FEAT]) for q in range(POOLED)]
        parts = sb("parts", [TILE, BLOCKS, PARTS, FEAT], BF16)
        src_hot = sb("src_hot", [TILE, RING, DEDGES], BF16)
        dense_rows = [sb(f"dense_rows{d}", [TILE, GROUP, PARTS * FEAT], BF16) for d in range(DENSE)]
        dst_hot = [sb(f"dst_hot{q}", [TILE, GROUP, WINDOW], F32 if q < POOLED else BF16) for q in range(UNIT)]

        psum = ctx.enter_context(nc.psum_tensor("psum", [128, 8, BANK], F32))
        weights_ps = [psum[:TILE, 0:5, :].rearrange("p k n -> p (k n)")[:, s * GROUP * WCOLS:(s + 1) * GROUP * WCOLS]
                      .rearrange("p (t n) -> p t n", t=GROUP) for s in range(2)]
        SHARED = [GROUP - 1, 0]
        FIRST = (GROUP - 1) * TILE
        hid_ps = [(0, FIRST, psum[:HID0, 5, 0:FIRST]), (FIRST, GEDGES, psum[:HID0, 6, 0:TILE])]
        window_ps = [psum[:, 7, 0:WINDOW]] * 2
        dense_ps = [psum[:TILE, d, 0:GROUP * PARTS * FEAT].rearrange("p (t f) -> p t f", t=GROUP) for d in range(DENSE)]
        unit_ps = [psum[:FEAT, 2 + q, 0:WINDOW] for q in range(UNIT)]

        const_in_s = sem("const_in_s")
        graph_in = sem("graph_in")
        x_in_s = sem("x_in_s")
        par_in = sem("par_in")
        filled = sem("filled")
        si_zeroed = sem("si_zeroed")
        zeroed = sem("zeroed")
        span_ready = sem("span_ready")
        diag_ready = sem("diag_ready")
        diag_summed = sem("diag_summed")
        var_ready = [sem(f"var_ready{k}") for k in range(2)]
        std_ready = [sem(f"std_ready{k}") for k in range(2)]
        h_ready = [sem(f"h_ready{k}") for k in range(2)]
        table_in = [sem(f"table_in{ph}") for ph in range(3)]
        h_turned = [sem(f"h_turned{k}") for k in range(2)]
        h_t_ready = [sem(f"h_t_ready{k}") for k in range(2)]
        out0_summed = sem("out0_summed")
        inv_ready = sem("inv_ready")
        inv_turned = sem("inv_turned")
        inv_deg_ready = sem("inv_deg_ready")
        mean_ready = [sem(f"mean_ready{k}") for k in range(2)]
        sage1_summed = sem("sage1_summed")
        h1_ready = sem("h1_ready")
        y_summed = sem("y_summed")
        y_ready = sem("y_ready")
        agg_turned = sem("agg_turned")
        out_ready = sem("out_ready")
        out_stored = sem("out_stored")
        step_dve = sem("step_dve")
        src_copied = sem("src_copied")
        gathered = [sem(f"gathered{s}") for s in range(2)]
        d_read = sem("d_read")
        d_ready = sem("d_ready")
        factors_ready = sem("factors_ready")
        away = sem("away")
        hot_ready = sem("hot_ready")
        summed = [sem(f"summed{ph}") for ph in range(3)]
        added = [sem(f"added{ph}") for ph in range(3)]
        src_raw_in = [sem(f"src_raw_in{s}") for s in range(2)]
        src16_ready = sem("src16_ready")
        pool_src_ready = [[sem(f"pool_src_ready{ph}{q}") for q in range(POOLED)] for ph in (1, 2)]
        pool_in = [[sem(f"pool_in{ph}{q}") for q in range(POOLED)] for ph in (1, 2)]
        parts_ready = [sem(f"parts_ready{ph}") for ph in (1, 2)]
        src_hot_ready = [sem(f"src_hot_ready{ph}") for ph in (1, 2)]
        block_summed = [sem(f"block_summed{ph}") for ph in (1, 2)]
        far = [sem(f"far{ph}") for ph in (1, 2)]
        dense_out = [sem(f"dense_out{ph}") for ph in (1, 2)]
        dst_hot_ready = [sem(f"dst_hot_ready{ph}") for ph in (1, 2)]
        base_ready = [sem(f"base_ready{ph}") for ph in range(3)]
        ef_in = [sem(f"ef_in{s}") for s in range(2)]
        hid_summed = sem("hid_summed")
        hid_ready = sem("hid_ready")
        weights_ready = sem("weights_ready")
        weights_read = sem("weights_read")
        products_summed = sem("products_summed")
        msg_ready = sem("msg_ready")

        PARS = 0

        def passes(eng):
            eng.wait_ge(span_ready, 1)
            span = eng.value_load(span_i[0:1, 0:1], min_val=0, max_val=NODES - 1)
            return eng.snap((span >> SHIFT) + 1, min_val=1, max_val=(NODES - 1) // WINDOW + 1)

        def group_of(n0, u, i):
            return i, n0 + i, i % 2, u[i % 2] + i // 2, i >= 1, i >= 2

        def over_groups(eng, n_pass, lead, step, tail, begin=None):
            with eng.Fori(0, n_pass) as j:
                if begin is not None:
                    begin(j)
                n0 = eng.snap(j * GROUPS)
                u = [eng.snap(j * USES[s]) for s in range(2)]
                at = lambda i: (lambda k: group_of(n0, u, i + k) if 0 <= i + k < GROUPS else None)
                lead(at(0))
                for s in range(2):
                    step(at(s))
                with eng.Fori(1, BODIES) as b:
                    g = eng.snap(b * 2)
                    n = eng.snap(n0 + g)
                    for s in range(2):
                        step(lambda k, s=s: (g + (s + k), n + (s + k), (s + k) % 2, u[(s + k) % 2] + b + (s + k) // 2,
                                             2 + s + k >= 1, 2 + s + k >= 2))
                step(at(GROUPS - 1))
                tail(at(GROUPS), j)

        def nothing(group):
            pass

        def over_units(eng, n_pass, lead, unit, tail, begin=None):
            with eng.Fori(0, n_pass) as j:
                if begin is not None:
                    begin(j)
                n0 = eng.snap(j * UNITS_OF)
                lead(n0)
                unit(0, n0, True, False)
                with eng.Fori(1, UNITS_OF - 1) as u:
                    unit(u, eng.snap(n0 + u), False, False)
                unit(UNITS_OF - 1, eng.snap(n0 + (UNITS_OF - 1)), False, True)
                tail(j, eng.snap(n0 + UNITS_OF))

        ORDER = [0, 1, 3, 4, 2]
        def turn(n, q):
            return n * UNIT + (1 + ORDER.index(q))

        def of_block(t, b):
            return t[:, b:b + (TILE - 1) * BLOCKS + 1:BLOCKS]

        block = ctx.enter_context(nc.Block())

        @block.sync
        def _(sp):
            sp.dma_start(const[:, :], const_in).then_inc(const_in_s, 16)
            sp.dma_start(dstg_raw[:, :], dst_groups_in).then_inc(graph_in, 16)
            sp.dma_start(x[:, :, :], x_in.rearrange("(p b) f -> p b f", b=BLOCKS)).then_inc(x_in_s, 16)
            sp.dma_start(dst_raw[:, :], dst_tiles_in).then_inc(graph_in, 16)
            sp.dma_start(src_all[:, :], src_in.bitcast(U32)).then_inc(graph_in, 16)
            sp.dma_start(sh_all[:, :, :], sh_in).then_inc(graph_in, 16)
            sp.wait_ge(si_zeroed, 1)
            sp.dma_start(si[0:MUL, 0:MUL], si0_in).then_inc(par_in, 16)
            for m in range(3):
                sp.dma_start(si[MUL * (m + 1):MUL * (m + 2), MUL + m:MUL + m + 3 * MUL - 2:3], si1_in,
                             allow_slow_non_contiguous=True).then_inc(par_in, 16)
            n_pass = passes(sp)
            sp.wait_ge(zeroed, 1)

            def load_edges(group):
                i, n, s, use, _, third = group(0)
                if third:
                    sp.wait_ge(hid_summed, n - 1)
                if third:
                    sp.wait_ge(src16_ready, n - 1)
                sp.dma_start(src_raw[s][:, :], src_dense_in[bass.ds(i, 1), :].broadcast_to([128, PIECE])
                             ).then_inc(src_raw_in[s], 16)
                sp.dma_start(ef[s][0:FEAT, :], ef_t_in[:, bass.ds(i * GEDGES, GEDGES)]).then_inc(ef_in[s], 16)

            def end(group, j):
                sp.wait_ge(added[0], (j + 1) * GROUPS)

            over_groups(sp, n_pass, nothing, load_edges, end)
            sp.wait_ge(out_stored, 16)

        @block.gpsimd
        def _(pool):
            nc.gpsimd.memset(si[:, :], 0.0).then_inc(si_zeroed, 1)
            n_pass = passes(pool)
            def gather(group):
                i, n, s, use, _, third = group(0)
                pool.wait_ge(src_copied, n + 1)
                if third:
                    pool.wait_ge(d_read, n - 1)
                    pool.wait_ge(factors_ready, n - 1)
                pool.wait_ge(table_in[0], 16)
                pool.nop(nofuse=True)
                for t in range(GROUP):
                    pool.indirect_dma_start(
                        out=gath[s][:, t, :], out_offset=None, in_=tables[0],
                        in_offset=bass.IndirectOffsetOnAxis(ap=src_slot[s][:, t:t + 1], axis=0),
                    ).then_inc(gathered[s], 16)

            def end(group, j):
                pool.wait_ge(added[0], (j + 1) * GROUPS)

            over_groups(pool, n_pass, nothing, gather, end)

            for ph in (1, 2):
                def unit(u, n, first, last, ph=ph):
                    for q in range(POOLED):
                        pool.wait_ge(pool_src_ready[ph - 1][q], n + 1)
                        if not first:
                            pool.wait_ge(summed[ph], turn(n - 1, q))
                        pool.wait_ge(table_in[ph], 16)
                        pool.nop(nofuse=True)
                        for t in range(GROUP):
                            pool.indirect_dma_start(
                                out=pool_rows[q][:, t, :], out_offset=None, in_=tables[ph],
                                in_offset=bass.IndirectOffsetOnAxis(ap=pool_src[q][:, t:t + 1], axis=0),
                            ).then_inc(pool_in[ph - 1][q], 16)

                def end(j, n, ph=ph):
                    pool.wait_ge(added[ph], n * UNIT)

                over_units(pool, n_pass, nothing, unit, end)

        @block.scalar
        def _(act):
            act.wait_ge(zeroed, 1)
            act.dma_start(w1[0:FEAT, :], w1_in).then_inc(par_in, 16)
            act.dma_start(b1[:, :], b1_in).then_inc(par_in, 16)
            act.dma_start(w2[0:HID0 + 1, :], w2_in).then_inc(par_in, 16)
            act.dma_start(sage1[:, :], sage1_in).then_inc(par_in, 16)
            act.dma_start(sage1_b[:, :], sage1_b_in).then_inc(par_in, 16)
            act.dma_start(sage2[:, :], sage2_in).then_inc(par_in, 16)
            act.dma_start(sage2_b[:, :], sage2_b_in.broadcast_to([TILE, FEAT])).then_inc(par_in, 16)
            act.wait_ge(filled, 1)

            def turned_out(to):
                to = to.rearrange("f (p b) -> f b p", b=BLOCKS)
                for c in range(0, BLOCKS, 4):
                    w = min(4, BLOCKS - c)
                    last = nc.scalar.copy(to[:, c:c + w, :],
                                          psum[:FEAT, c // 4, 0:w * TILE].rearrange("f (b p) -> f b p", b=w))
                return last

            def std_and_table(k):
                act.wait_ge(var_ready[k], 1)
                nc.scalar.activation(stat[:, 2, :], stat[:, 1, :], ACT.Sqrt, bias=eps[:TILE, :],
                                     scale=1.0 / FEAT).then_inc(std_ready[k], 1)
                act.wait_ge(h_ready[k], 1)
                act.dma_start(tables[k].rearrange("(p b) f -> p b f", b=BLOCKS), h[:, :, :]).then_inc(table_in[k], 16)
                act.wait_ge(h_turned[k], 1)
                turned_out(h_t[:, :] if k == 0 else stack[FEAT:2 * FEAT, 0:NODES]).then_inc(h_t_ready[k], 1)

            std_and_table(0)
            n_pass = passes(act)
            act.wait_ge(par_in, 16 * 11)
            act.wait_ge(graph_in, 64)
            def copy_src(group):
                i, n, s, use, _, third = group
                if third:
                    act.wait_ge(gathered[s], use * (16 * GROUP))
                nc.scalar.copy(src_slot[s][:, :], src_all[:, bass.ds(i * GROUP, GROUP)]).then_inc(src_copied, 1)

            def narrow_src(group):
                i, n, s, use, _, third = group(0)
                act.wait_ge(src_raw_in[s], (use + 1) * 16)
                nc.scalar.copy(src16[:, bass.ds(i * PIECE, PIECE)], src_raw[s][:, :]).then_inc(src16_ready, 1)

            def relu(group):
                i, n, s, use, _, third = group
                act.wait_ge(hid_summed, n + 1)
                if third:
                    act.wait_ge(weights_ready, n - 1)
                for a, z, ps in hid_ps:
                    last = nc.scalar.activation(hid[s][0:HID0, a:z], ps, ACT.Relu, bias=b1[:, 0:1])
                last.then_inc(hid_ready, 1)

            def distances(to, i):
                for t in range(GROUP):
                    last = nc.scalar.activation(to[:, t, :], iota[:TILE, :], ACT.Abs,
                                                bias=dst_rel[:, bass.ds(i * GROUP + t, 1)])
                return last

            def one_hot(to, of):
                return nc.scalar.activation(to, of, ACT.Relu, bias=1.0, scale=-1.0)

            def group_one_hot(group):
                i, n, s, use, _, third = group
                if third:
                    act.wait_ge(hot_ready, n - 1)
                distances(distance[s], i).then_inc(away, 1)
                if third:
                    act.wait_ge(summed[0], n - 1)
                act.wait_ge(away, n + 1)
                one_hot(hot[s][:, :, :], distance[s][:, :, :]).then_inc(hot_ready, 1)

            def factors(group):
                i, n, s, use, _, third = group
                act.wait_ge(gathered[s], (use + 1) * (16 * GROUP))
                if third:
                    act.wait_ge(weights_read, n - 1)
                for t in range(GROUP):
                    nc.scalar.activation(z_av[s][:, t, :], gath[s][:, t, :], ACT.Copy,
                                         scale=sh_all[:, bass.ds(i * GROUP + t, 1), 0])
                nc.scalar.copy(z_sd[s][:, :, 0, :], gath[s][:, :, 0:MUL]).then_inc(factors_ready, 1)

            def ahead(group):
                relu(group(0))
                if group(-1) is not None:
                    factors(group(-1))
                    if group(1) is not None:
                        copy_src(group(1))
                    group_one_hot(group(-1))
                narrow_src(group)

            def lead(group):
                copy_src(group(0))
                copy_src(group(1))

            def begin(j):
                act.wait_ge(base_ready[0], j * 2 + 1)

            def end(group, j):
                factors(group(-1))
                group_one_hot(group(-1))
                act.wait_ge(added[0], (j + 1) * GROUPS)

            over_groups(act, n_pass, lead, ahead, end, begin)
            std_and_table(1)
            act.wait_ge(inv_turned, 1)
            turned_out(inv_deg[:, :]).then_inc(inv_deg_ready, 1)

            for ph in (1, 2):
                def copy_pool_src(u, n, q, first, ph=ph):
                    if not first:
                        act.wait_ge(pool_in[ph - 1][q], n * (16 * GROUP))
                    nc.scalar.copy(pool_src[q][:, :], src_all[:, bass.ds((u * UNIT + q) * GROUP, GROUP)]
                                   ).then_inc(pool_src_ready[ph - 1][q], 1)

                def target_hot(u, n, q, first, ph=ph):
                    k = ORDER.index(q)
                    i = u * UNIT + q
                    d = distance[k % 2]
                    if k >= 2:
                        act.wait_ge(dst_hot_ready[ph - 1], n * UNIT + (k - 1))
                    elif not first:
                        act.wait_ge(dst_hot_ready[ph - 1], n * UNIT)
                    distances(d, i).then_inc(far[ph - 1], 1)
                    if not first:
                        act.wait_ge(summed[ph], turn(n - 1, q))
                    act.wait_ge(far[ph - 1], turn(n, q))
                    one_hot(dst_hot[q][:, :, :], d[:, :, :]).then_inc(dst_hot_ready[ph - 1], 1)

                def unit(u, n, first, last, ph=ph):
                    for q in (0, 1, 3, 4):
                        target_hot(u, n, q, first)
                    copy_pool_src(u, n, 2, first)
                    target_hot(u, n, 2, first)
                    if not last:
                        for q in (0, 1):
                            copy_pool_src(u + 1, n + 1, q, False)
                    act.wait_ge(block_summed[ph - 1], (n + 1) * BLOCKS)
                    for d in range(DENSE):
                        if not first:
                            act.wait_ge(summed[ph], turn(n - 1, POOLED + d))
                        nc.scalar.copy(dense_rows[d][:, :, :], dense_ps[d]).then_inc(dense_out[ph - 1], 1)

                def begin(j, ph=ph):
                    act.wait_ge(base_ready[ph], j * 2 + 1)

                def lead(n, ph=ph):
                    for q in (0, 1):
                        copy_pool_src(0, n, q, True)

                def end(j, n, ph=ph):
                    act.wait_ge(added[ph], n * UNIT)

                over_units(act, n_pass, lead, unit, end, begin)
                if ph == 1:
                    act.wait_ge(sage1_summed, 1)
                    for k, a in enumerate(range(0, NODES, CHUNK)):
                        w = min(CHUNK, NODES - a)
                        last = nc.scalar.activation(h1_t[:, a:a + w], psum[:HID1, k, 0:w], ACT.Relu,
                                                    bias=sage1_b[:, 0:1])
                    last.then_inc(h1_ready, 1)
                    act.wait_ge(y_ready, 1)
                    act.dma_start(tables[2].rearrange("(p b) f -> p b f", b=BLOCKS), h[:, :, :]).then_inc(table_in[2], 16)
            act.wait_ge(out_ready, 1)
            act.dma_start(out.rearrange("(p b) f -> p b f", b=BLOCKS), h[:, :, :]).then_inc(out_stored, 16)

        @block.tensor
        def _(pe):
            pe.wait_ge(diag_ready, 1)
            nc.tensor.matmul(psum[:, 7, 0:2 * GROUPS], ones[0:GROUPS, :], diag[:, :, :], start=True,
                             stop=True).then_inc(diag_summed, 1)

            def turn_h(k):
                pe.wait_ge(h_ready[k], 1)
                for b in range(BLOCKS):
                    last = nc.tensor.transpose(psum[:FEAT, b // 4, (b % 4) * TILE:(b % 4 + 1) * TILE], h[:, b, :],
                                               ident[:TILE, :TILE])
                last.then_inc(h_turned[k], 1)

            turn_h(0)
            n_pass = passes(pe)
            pe.wait_ge(par_in, 16 * 11)
            pe.wait_ge(filled, 1)
            pe.wait_ge(h_t_ready[0], 1)
            for ph in range(3):
                def hidden(group):
                    i, n, s, use, second, third = group
                    pe.wait_ge(ef_in[s], (use + 1) * 16)
                    if second:
                        pe.wait_ge(hid_ready, n)
                    for a, z, ps in hid_ps:
                        last = nc.tensor.matmul(ps, w1[:, :], ef[s][:, a:z], start=True, stop=True)
                    last.then_inc(hid_summed, 1)

                def weights(group):
                    i, n, s, use, second, third = group
                    pe.wait_ge(hid_ready, n + 1)
                    if third:
                        pe.wait_ge(weights_read, n - 1)
                    for t in sorted(range(GROUP), key=lambda t: t == SHARED[s]):
                        if t == SHARED[s] and second:
                            pe.wait_ge(weights_read, n)
                        last = nc.tensor.matmul(weights_ps[s][:, t, :], hid[s][:, t * TILE:(t + 1) * TILE], w2[:, :],
                                                start=True, stop=True)
                    last.then_inc(weights_ready, 1)

                def window(group):
                    i, n, s, use, second, third = group
                    pe.wait_ge(msg_ready, n + 1)
                    pe.wait_ge(hot_ready, n + 1)
                    if second:
                        pe.wait_ge(added[0], n)
                    for t in range(GROUP):
                        last = nc.tensor.matmul(window_ps[s], msg[s][:, t, :], hot[s][:, t, :],
                                                start=(t == 0), stop=(t == GROUP - 1))
                    last.then_inc(summed[0], 1)

                def end(group, j, ph=ph):
                    pe.wait_ge(added[ph], (j + 1) * GROUPS)

                if ph == 0:
                    def ahead(group):
                        if group(2) is not None:
                            hidden(group(2))
                        if group(1) is not None:
                            weights(group(1))
                        window(group(0))

                    def lead(group):
                        hidden(group(0))
                        hidden(group(1))
                        weights(group(0))

                    with pe.Fori(0, n_pass) as j:
                        n0 = pe.snap(j * GROUPS)
                        u = [pe.snap(j * USES[s]) for s in range(2)]
                        at = lambda i: (lambda k: group_of(n0, u, i + k) if 0 <= i + k < GROUPS else None)
                        lead(at(0))
                        ahead(at(0))
                        with pe.Fori(1, BODIES) as b:
                            n = pe.snap(n0 + b * 2)
                            for s in (-1, 0):
                                ahead(lambda k, s=s: (None, n + (s + k), (s + k) % 2,
                                                      u[(s + k) % 2] + b + (s + k) // 2, 2 + s + k >= 1, 2 + s + k >= 2))
                        ahead(at(GROUPS - 2))
                        ahead(at(GROUPS - 1))
                        end(None, j)
                    for b in range(BLOCKS):
                        to = psum[:TILE, b // OUT0_BLOCKS, (b % OUT0_BLOCKS) * OUT0:(b % OUT0_BLOCKS + 1) * OUT0]
                        nc.tensor.matmul(to, of_block(acc, b), fold, start=True, stop=False)
                        last = nc.tensor.matmul(to[:, 0:FEAT], of_block(h_t, b), si[:, :], start=False, stop=True)
                    last.then_inc(out0_summed, 1)
                    turn_h(1)
                    pe.wait_ge(h_t_ready[1], 1)
                    pe.wait_ge(inv_ready, 1)
                    for b in range(BLOCKS):
                        last = nc.tensor.matmul(psum[:FEAT, b // 4, (b % 4) * TILE:(b % 4 + 1) * TILE],
                                                inv[:, b:b + 1].to_broadcast([TILE, FEAT]), ident[:TILE, :TILE],
                                                start=True, stop=True)
                    last.then_inc(inv_turned, 1)
                    pe.wait_ge(inv_deg_ready, 1)
                else:
                    def block_sums(u, n, b, ph=ph):
                        pe.wait_ge(src_hot_ready[ph - 1], n * BLOCKS + (b + 1))
                        for d in range(DENSE):
                            for t in range(GROUP):
                                at = (d * GROUP + t) * TILE
                                last = nc.tensor.matmul(dense_ps[d][:, t, :], src_hot[:, b % RING, at:at + TILE],
                                                        parts[:, b, :, :].rearrange("p k f -> p (k f)"),
                                                        start=(b == 0 and t == 0), stop=(b == BLOCKS - 1),
                                                        skip_group_check=True)
                        last.then_inc(block_summed[ph - 1], 1)

                    def unit_window(n, q, first, ph=ph):
                        pe.wait_ge(dst_hot_ready[ph - 1], turn(n, q))
                        if not first:
                            pe.wait_ge(added[ph], turn(n - 1, q))
                        if q < POOLED:
                            pe.wait_ge(pool_in[ph - 1][q], (n + 1) * (16 * GROUP))
                            rows = [(t, pool_rows[q][:, t, :]) for t in range(GROUP)]
                        else:
                            d = q - POOLED
                            pe.wait_ge(dense_out[ph - 1], n * DENSE + (d + 1))
                            rows = [(t, dense_rows[d][:, t, k * FEAT:(k + 1) * FEAT])
                                    for t in range(GROUP) for k in range(PARTS)]
                        for k, (t, row) in enumerate(rows):
                            last = nc.tensor.matmul(unit_ps[q], row, dst_hot[q][:, t, :], start=(k == 0),
                                                    stop=(k == len(rows) - 1))
                        last.then_inc(summed[ph], 1)

                    def unit(u, n, first, last, ph=ph):
                        for b in range(BLOCKS):
                            block_sums(u, n, b)
                            if b == 5 and not first:
                                late_window(n)
                            if b == 12:
                                unit_window(n, 0, first)
                        for q in (1, 3, 4):
                            unit_window(n, q, first)

                    def late_window(n, ph=ph):
                        pe.wait_ge(dst_hot_ready[ph - 1], turn(n - 1, 2))
                        pe.wait_ge(added[ph], turn(n - 1, 0))
                        pe.wait_ge(pool_in[ph - 1][2], n * (16 * GROUP))
                        for t in range(GROUP):
                            last = nc.tensor.matmul(unit_ps[2], pool_rows[2][:, t, :], dst_hot[2][:, t, :],
                                                    start=(t == 0), stop=(t == GROUP - 1))
                        last.then_inc(summed[ph], 1)

                    def unit_end(j, n, ph=ph):
                        late_window(n)
                        pe.wait_ge(added[ph], n * UNIT)

                    pe.wait_ge(parts_ready[ph - 1], 1)
                    over_units(pe, n_pass, nothing, unit, unit_end)
                    pe.wait_ge(mean_ready[ph - 1], 1)
                    if ph == 1:
                        for k, a in enumerate(range(0, NODES, CHUNK)):
                            w = min(CHUNK, NODES - a)
                            last = nc.tensor.matmul(psum[:HID1, k, 0:w], sage1[:, :], stack[:, a:a + w], start=True,
                                                    stop=True)
                        last.then_inc(sage1_summed, 1)
                        pe.wait_ge(h1_ready, 1)
                        for b in range(BLOCKS):
                            last = nc.tensor.matmul(psum[:TILE, b // 8, (b % 8) * 2 * FEAT:(b % 8 + 1) * 2 * FEAT],
                                                    of_block(h1_t, b), sage2[:, :], start=True, stop=True)
                        last.then_inc(y_summed, 1)
                        pe.wait_ge(y_ready, 1)
                    else:
                        for b in range(BLOCKS):
                            last = nc.tensor.matmul(psum[:TILE, b // 16, (b % 16) * FEAT:(b % 16 + 1) * FEAT],
                                                    of_block(stack[0:FEAT, :], b), ident[:FEAT, :FEAT], start=True,
                                                    stop=True)
                        last.then_inc(agg_turned, 1)

        @block.vector
        def _(dve):
            vec = nc.vector
            steps = [0]

            def done(ins):
                steps[0] += 1
                ins.then_inc(step_dve, 1)
                dve.wait_ge(step_dve, steps[0])

            vec.memset(w1[:, :], 0.0)
            for s in range(2):
                vec.memset(ef[s][:, :], 0.0)
            vec.memset(w2[:, :], 0.0).then_inc(zeroed, 1)
            vec.memset(eps[:, :], EPS)
            vec.memset(ones[:, :], 1.0)
            vec.memset(acc[:, :], 0.0)
            for s in range(2):
                vec.memset(msg[s][:, :, SH_SUMS:DEG], 0.0)
                vec.memset(msg[s][:, :, DEG:128], 1.0)
                done(vec.memset(hid[s][HID0:128, :], 0.0))
                last = vec.memset(hid[s][HID0:HID0 + 1, :], 1.0)
            last.then_inc(filled, 1)

            dve.wait_ge(const_in_s, 16)
            dve.wait_ge(const_in_s, 16)
            dve.wait_ge(graph_in, 64)
            done(vec.tensor_copy(dstg_f[:, :], dstg_raw[:, :]))
            vec.tensor_reduce(low_high[:, 0:1], dstg_f[:, :], AX_X, ALU.min)
            done(vec.tensor_reduce(low_high[:, 1:2], dstg_f[:, :], AX_X, ALU.max))
            done(vec.tensor_tensor(low_high[:, 2:3], low_high[:, 1:2], low_high[:, 0:1], ALU.subtract))
            vec.tensor_scalar(diag[:, 0, :], ident[:GROUPS, :GROUPS], low_high[:, 0:1], None, ALU.mult)
            vec.tensor_scalar(diag[:, 1, :], ident[:GROUPS, :GROUPS], low_high[:, 2:3], None,
                              ALU.mult).then_inc(diag_ready, 1)
            dve.wait_ge(diag_summed, 1)
            done(vec.tensor_copy(base0[:, :, :], psum[:, 7, 0:2 * GROUPS].rearrange("p (k g) -> p k g", k=2)))
            done(vec.tensor_reduce(span_f[:, :], base0[0:1, 1, :], AX_X, ALU.max))
            vec.tensor_copy(span_i[:, :], span_f[:, :]).then_inc(span_ready, 1)
            vec.tensor_copy(dst_f[:, :], dst_raw[:, :])
            vec.tensor_scalar(shc_all[:, :, :], sh_all[:, :, 1:4], float(C110), None, ALU.mult)
            dve.wait_ge(par_in, 16 * 11)
            done(vec.tensor_scalar(si[:, :], si[:, :], float(SI_SCALE), None, ALU.mult))

            def layernorm_relu(k):
                done(vec.tensor_reduce(stat[:, 0, :], x[:, :, :], AX_X, ALU.add))
                done(vec.tensor_scalar(stat[:, 0, :], stat[:, 0, :], 1.0 / FEAT, None, ALU.mult))
                done(vec.tensor_tensor(xc[:, :, :], x[:, :, :], stat[:, 0, :].broadcast_to_dim(FEAT)
                                       if False else spread(stat[:, 0, :], FEAT), ALU.subtract))
                done(vec.tensor_tensor(sq[:, :, :], xc[:, :, :], xc[:, :, :], ALU.mult))
                vec.tensor_reduce(stat[:, 1, :], sq[:, :, :], AX_X, ALU.add).then_inc(var_ready[k], 1)
                dve.wait_ge(std_ready[k], 1)
                done(vec.reciprocal(stat[:, 3, :], stat[:, 2, :]))
                done(vec.tensor_tensor(xc[:, :, :], xc[:, :, :], spread(stat[:, 3, :], FEAT), ALU.mult))
                if k == 0:
                    vec.tensor_scalar(h[:, :, 0:MUL], xc[:, :, 0:MUL], 0.0, None, ALU.max)
                    vec.tensor_scalar(h[:, :, MUL:FEAT].rearrange("p b (m i) -> p b m i", m=3),
                                      xc[:, :, MUL:FEAT].rearrange("p b (i m) -> p b m i", m=3), 0.0, None,
                                      ALU.max).then_inc(h_ready[k], 1)
                else:
                    vec.tensor_scalar(h[:, :, :], xc[:, :, :], 0.0, None, ALU.max).then_inc(h_ready[k], 1)

            def spread(a, n):
                return a.unsqueeze(2).to_broadcast([a.shape[0], a.shape[1], n])

            dve.wait_ge(x_in_s, 16)
            layernorm_relu(0)
            n_pass = passes(dve)

            def place_windows(ph, j, sums):
                vec.tensor_tensor(dst_rel[:, :].rearrange("p (g t) -> p g t", t=GROUP), spread(base[:TILE, :], GROUP),
                                  dst_f[:, :].rearrange("p (g t) -> p g t", t=GROUP), ALU.subtract)
                vec.tensor_copy(base_row[:, :], base[0:1, :]).then_inc(base_ready[ph], 1)
                dve.wait_ge(base_ready[ph], j * 2 + 1)

            def move_windows(ph, j):
                dve.wait_ge(added[ph], (j + 1) * GROUPS)
                vec.tensor_scalar(base[:, :], base[:, :], float(WINDOW), float(NODES), ALU.add,
                                  ALU.min).then_inc(base_ready[ph], 1)
                dve.wait_ge(base_ready[ph], j * 2 + 2)

            def add_window(ph, group, sums, behind=False):
                i, n, s, use, _, _ = group
                at = dve.value_load(base_row[0:1, bass.ds(i, 1)], min_val=0, max_val=NODES)
                dve.wait_ge(summed[ph], n + 1)
                if behind:
                    dve.wait_ge(added[ph], n)
                to = sums[:, bass.ds(at, WINDOW)]
                vec.tensor_tensor(to, to, window_ps[s], ALU.add).then_inc(added[ph], 1)

            def factor_d(group):
                i, n, s, use, _, _ = group
                shc = shc_all[:, bass.ds(i * GROUP, GROUP), :]
                dve.wait_ge(gathered[s], (use + 1) * (16 * GROUP))
                vec.tensor_tensor(dprod[:, :, :, :], gath[s][:, :, MUL:FEAT].rearrange("p t (m i) -> p t m i", m=3),
                                  shc.unsqueeze(3).to_broadcast([TILE, GROUP, 3, MUL]), ALU.mult).then_inc(d_read, 1)

            def sum_factor_d(group):
                i, n, s, use, _, _ = group
                dve.wait_ge(d_read, n + 1)
                vec.tensor_reduce(z_sd[s][:, :, 1, :], dprod[:, :, :, :].rearrange("p t m i -> p t i m"), AX_X,
                                  ALU.add).then_inc(d_ready, 1)

            def products(group):
                i, n, s, use, _, _ = group
                w = weights_ps[s]
                dve.wait_ge(d_ready, n + 1)
                dve.wait_ge(factors_ready, n + 1)
                dve.wait_ge(weights_ready, n + 1)
                vec.tensor_tensor(prod[:, :, 0, :, :], w[:, :, 0:64].rearrange("p t (i o) -> p t i o", i=MUL),
                                  z_av[s][:, :, 0:MUL].unsqueeze(3).to_broadcast([TILE, GROUP, MUL, MUL]), ALU.mult)
                vec.tensor_tensor(
                    prod[:, :, 1:4, :, :].rearrange("p t m i o -> p t (m i) o"),
                    w[:, :, 64:128].rearrange("p t (m n) -> p t m n", m=1).to_broadcast([TILE, GROUP, 3, 64]),
                    z_av[s][:, :, MUL:FEAT].unsqueeze(3).to_broadcast([TILE, GROUP, 3 * MUL, MUL]), ALU.mult)
                vec.tensor_tensor(prod[:, :, 4:6, :, :].rearrange("p t c i o -> p t (c i) o"),
                                  w[:, :, 128:256].rearrange("p t (i o) -> p t i o", o=MUL),
                                  z_sd[s][:, :, :, :].rearrange("p t c i -> p t (c i)").unsqueeze(3)
                                  .to_broadcast([TILE, GROUP, 2 * MUL, MUL]), ALU.mult).then_inc(weights_read, 1)

            def sum_products(group):
                i, n, s, use, _, third = group
                if third:
                    dve.wait_ge(summed[0], n - 1)
                dve.wait_ge(weights_read, n + 1)
                vec.tensor_reduce(msg[s][:, :, 0:SUMS].rearrange("p t (c o) -> p t c o", c=UNITS),
                                  prod[:, :, :, :, :].rearrange("p t c i o -> p t c o i"), AX_X,
                                  ALU.add).then_inc(products_summed, 1)

            def times_sh1(group):
                i, n, s, use, _, _ = group
                dve.wait_ge(products_summed, n + 1)
                vec.tensor_tensor(msg[s][:, :, SUMS:SH_SUMS].rearrange("p t (m o) -> p t m o", m=3),
                                  msg[s][:, :, 4 * MUL:5 * MUL].unsqueeze(2).to_broadcast([TILE, GROUP, 3, MUL]),
                                  sh_all[:, bass.ds(i * GROUP, GROUP), 1:4].unsqueeze(3)
                                  .to_broadcast([TILE, GROUP, 3, MUL]), ALU.mult).then_inc(msg_ready, 1)

            def messages(group):
                sum_factor_d(group(0))
                if group(-2) is not None:
                    add_window(0, group(-2), acc)
                if group(-1) is not None:
                    times_sh1(group(-1))
                products(group(0))
                if group(1) is not None:
                    factor_d(group(1))
                sum_products(group(0))

            for ph in range(3):
                sums = acc if ph == 0 else stack[0:FEAT, :]
                if ph:
                    vec.memset(sums[:, :], 0.0)
                done(vec.tensor_copy(base[:, :], base0[:, 0, :]))
                if ph == 0:
                    def begin(j):
                        place_windows(0, j, acc)

                    def lead(group):
                        factor_d(group(0))

                    def end(group, j):
                        add_window(0, group(-2), acc)
                        times_sh1(group(-1))
                        add_window(0, group(-1), acc, behind=True)
                        move_windows(0, j)

                    over_groups(dve, n_pass, lead, messages, end, begin)
                    dve.wait_ge(out0_summed, 1)
                    for k, (a, z) in enumerate(((0, OUT0_BLOCKS), (OUT0_BLOCKS, BLOCKS))):
                        got = psum[:TILE, k, 0:(z - a) * OUT0].rearrange("p (b f) -> p b f", f=OUT0)
                        last = vec.tensor_tensor(x[:, a:z, :], x[:, a:z, :], got[:, :, 0:FEAT], ALU.add)
                        vec.tensor_scalar(degree[:, a:z], got[:, :, FEAT], 1.0, None, ALU.max)
                    steps[0] += 1
                    last.then_inc(step_dve, 1)
                    dve.wait_ge(step_dve, steps[0])
                    layernorm_relu(1)
                    vec.reciprocal(inv[:, :], degree[:, :]).then_inc(inv_ready, 1)
                else:
                    high, mid, low = (parts[:, :, k, :] for k in range(PARTS))
                    done(vec.tensor_copy(high, h[:, :, :]))
                    done(vec.tensor_tensor(xc[:, :, :], h[:, :, :], high, ALU.subtract))
                    done(vec.tensor_copy(mid, xc[:, :, :]))
                    vec.tensor_tensor(low, xc[:, :, :], mid, ALU.subtract).then_inc(parts_ready[ph - 1], 1)

                    def add_unit_window(u, n, q, first, ph=ph, sums=sums):
                        at = dve.value_load(base_row[0:1, bass.ds(u * UNIT + q, 1)], min_val=0, max_val=NODES)
                        dve.wait_ge(summed[ph], turn(n, q))
                        if not (first and q == 0):
                            dve.wait_ge(added[ph], turn(n, q) - 1)
                        to = sums[:, bass.ds(at, WINDOW)]
                        vec.tensor_tensor(to, to, unit_ps[q], ALU.add).then_inc(added[ph], 1)

                    def unit(u, n, first, last, ph=ph):
                        for b in range(BLOCKS):
                            if b >= RING or not first:
                                dve.wait_ge(block_summed[ph - 1], n * BLOCKS + (b + 1 - RING))
                            vec.tensor_scalar(src_hot[:, b % RING, :], src16[:TILE, bass.ds(u * DEDGES, DEDGES)],
                                              ids[:TILE, b:b + 1], None, ALU.is_equal).then_inc(src_hot_ready[ph - 1], 1)
                            if b in LATE and not first:
                                add_unit_window(u - 1, n - 1, LATE[b], False)
                            if b == 20:
                                add_unit_window(u, n, 0, first)

                    LATE = {2: 1, 4: 3, 6: 4, 11: 2}

                    def begin(j, ph=ph, sums=sums):
                        place_windows(ph, j, sums)

                    def end(j, n, ph=ph):
                        for q in (1, 3, 4, 2):
                            add_unit_window(UNITS_OF - 1, n - 1, q, False)
                        move_windows(ph, j)

                    over_units(dve, n_pass, nothing, unit, end, begin)
                    dve.wait_ge(inv_deg_ready, 1)
                    vec.tensor_tensor(sums[:, 0:NODES], sums[:, 0:NODES], inv_deg[:, :],
                                      ALU.mult).then_inc(mean_ready[ph - 1], 1)
                    if ph == 1:
                        dve.wait_ge(y_summed, 1)
                        for k, a in enumerate(range(0, BLOCKS, 8)):
                            z = min(a + 8, BLOCKS)
                            y = psum[:TILE, k, 0:(z - a) * 2 * FEAT].rearrange("p (b f) -> p b f", f=2 * FEAT)
                            vec.tensor_copy(h[:, a:z, :], y[:, :, 0:FEAT])
                            last = vec.tensor_tensor(x[:, a:z, :], x[:, a:z, :], y[:, :, FEAT:2 * FEAT], ALU.add)
                        done(last)
                        vec.tensor_tensor(x[:, :, :], x[:, :, :],
                                          sage2_b[:, :].unsqueeze(1).to_broadcast([TILE, BLOCKS, FEAT]),
                                          ALU.add).then_inc(y_ready, 1)
                    else:
                        dve.wait_ge(agg_turned, 1)
                        dve.wait_ge(table_in[2], 16)
                        for k, (a, z) in enumerate(((0, 16), (16, BLOCKS))):
                            last = vec.tensor_tensor(h[:, a:z, :], x[:, a:z, :],
                                                     psum[:TILE, k, 0:(z - a) * FEAT].rearrange(
                                                         "p (b f) -> p b f", f=FEAT), ALU.add)
                        last.then_inc(out_ready, 1)


def kernel(**inputs):
    import concourse.bacc as _bacc
    from concourse.bass_utils import run_bass_kernel_spmd as _run

    a = {k: np.asarray(v) for k, v in inputs.items()}
    order = [0, 2, 1, 3]
    w2 = np.concatenate([a["L0_gnn_W2"], a["L0_gnn_b2"][None]], axis=0).reshape(HID0 + 1, 4, MUL * MUL)[:, order]
    laid = {
        "x": a["x"],
        "src": a["src"].reshape(TILES, TILE).T,
        "src_dense": a["src"].reshape(UNITS_OF, UNIT, GEDGES)[:, POOLED:].reshape(GROUPS, PIECE),
        "dst_tiles": a["dst"].reshape(TILES, TILE).T,
        "dst_groups": a["dst"].reshape(GROUPS, GEDGES),
        "ef_t": a["edge_attr_32"].T,
        "sh": a["edge_attr_4"].reshape(TILES, TILE, 4).transpose(1, 0, 2),
        "w1": a["L0_gnn_W1"], "b1": a["L0_gnn_b1"].reshape(HID0, 1), "w2": w2.reshape(HID0 + 1, WCOLS),
        "si0": a["L0_gnn_si_w0"], "si1": a["L0_gnn_si_w1"],
        "sage1": np.concatenate([a["L1_gnn_W1_l"], a["L1_gnn_W1_r"]], axis=0),
        "sage1_b": a["L1_gnn_b1"].reshape(HID1, 1),
        "sage2": np.concatenate([a["L1_gnn_W2_l"], a["L1_gnn_W2_r"]], axis=1),
        "sage2_b": a["L1_gnn_b2"].reshape(1, FEAT),
        "const": constants(),
    }
    nc = _bacc.Bacc("TRN2", target_bir_lowering=False, num_devices=1)
    arrays, args = {}, []
    for name, v in laid.items():
        v = np.ascontiguousarray(v)
        arrays[f"in_{name}_dram"] = v
        args.append(nc.dram_tensor(f"in_{name}_dram", v.shape, mybir.dt.from_np(v.dtype), kind="ExternalInput").ap())
    args.append(nc.dram_tensor("out_dram", (NODES, FEAT), F32, kind="ExternalOutput").ap())
    gnn(nc, *args)
    r = _run(nc, [arrays], core_ids=[0])
    return r.results[0]["out_dram"]
```

```python
from contextlib import ExitStack

import numpy as np

import concourse.bass as bass
from concourse import mybir
from concourse.alu_op_type import AluOpType as ALU

F32 = mybir.dt.float32
I32 = mybir.dt.int32
I16 = mybir.dt.int16
BF16 = mybir.dt.bfloat16
F16 = mybir.dt.float16
U32 = mybir.dt.uint32
ACT = mybir.ActivationFunctionType
AX_X = mybir.AxisListType.X

NODES, EDGES, FEAT = 3125, 53125, 32
MUL = 8
HID0, HID1 = 64, 64
WCOLS = 4 * MUL * MUL
ALPHA, C110, SI_SCALE, EPS = 0.25, 1.0 / np.sqrt(3.0), 1.0 / np.sqrt(8.0), 1e-5

TILE = 125
BLOCKS = NODES // TILE
TILES = EDGES // TILE
GROUP = 5
GROUPS = TILES // GROUP
GEDGES = GROUP * TILE
WINDOW = 48
BODY = 2
BODIES = GROUPS // BODY
USES = [(GROUPS + 1) // 2, GROUPS // 2]
UNIT = 5
COUNTED, POOLED = (0, 1, 3), (2, 4)
ALL_UNITS = GROUPS // UNIT
COUNTED_TILES = len(COUNTED) * GROUP
COUNTS = BLOCKS * WINDOW
COUNT_CUTS = [0, 9 * WINDOW, 17 * WINDOW, COUNTS]
TURNED = 5
PARTS = 3
ROUND = float(3 << 22)
assert BLOCKS % TURNED == 0 and BLOCKS * TILE == NODES and TILES * TILE == EDGES and GROUPS * GROUP == TILES
assert GROUPS == BODIES * BODY + 1 and ALL_UNITS * UNIT == GROUPS

PATHS = 6
SUMS = PATHS * MUL
SH_SUMS = SUMS + 3 * MUL
DEG = SH_SUMS
ROWS = PARTS * FEAT
ACC = NODES + WINDOW
CHUNK = 500
BANK = 512


def constants():
    ident = np.eye(128, dtype=np.float32)
    iota = np.tile(np.arange(WINDOW, dtype=np.float32), (128, 1))
    return np.concatenate([ident, iota], axis=1)


def gnn(nc, x_in, src_in, dst_tiles_in, dst_groups_in, ef_t_in, sh_in, w1_in, b1_in, w2_in, si0_in, si1_in,
        sage1_in, sage1_b_in, sage2_in, sage2_b_in, const_in, columns_in, out):
    ctx = ExitStack()
    with ctx:
        def sb(name, shape, dt=F32):
            return ctx.enter_context(nc.sbuf_tensor(name, shape, dt))

        def sem(name):
            return ctx.enter_context(nc.semaphore(name))

        inv_row = nc.dram_tensor("inv_row", (1, NODES), F32, kind="Internal").ap()
        tables = [nc.dram_tensor(f"table{ph}", (NODES, FEAT), F32, kind="Internal").ap() for ph in range(3)]

        const = sb("const", [128, 128 + WINDOW])
        ident, iota = const[:, 0:128], const[:, 128:128 + WINDOW]
        columns = sb("columns", [128, COUNTS], I16)
        ones = sb("ones", [128, 128])
        eps = sb("eps", [128, 1])
        eps_root = sb("eps_root", [128, 1])
        w1 = sb("w1", [128, HID0])
        b1 = sb("b1", [HID0, 1])
        w2 = sb("w2", [128, WCOLS])
        si = sb("si", [128, FEAT])
        sage1 = sb("sage1", [128, HID1])
        sage1_b = sb("sage1_b", [HID1, 1])
        sage2 = sb("sage2", [128, 128])
        sage2_b = sb("sage2_b", [TILE, FEAT])
        src_all = sb("src_all", [TILE, TILES], U32)
        src_slot = [sb(f"src_slot{s}", [TILE, GROUP], U32) for s in range(2)]
        dst_raw = sb("dst_raw", [TILE, TILES], I32)
        dst_f = sb("dst_f", [TILE, TILES])
        dst_rel = sb("dst_rel", [TILE, TILES])
        dstg_raw = sb("dstg_raw", [GROUPS, GEDGES], I32)
        dstg_f = sb("dstg_f", [GROUPS, GEDGES])
        low_high = sb("low_high", [GROUPS, 3])
        diag = sb("diag", [GROUPS, 2, GROUPS])
        base0 = sb("base0", [128, 2, GROUPS])
        base = sb("base", [128, GROUPS])
        base_row = sb("base_row", [1, GROUPS], I32)
        span_f = sb("span_f", [1, 1])
        more_passes = sb("more_passes", [1, 1], I32)
        sh_all = sb("sh_all", [TILE, TILES, 4])
        shc_all = sb("shc_all", [TILE, TILES, 3])
        x = sb("x", [TILE, BLOCKS, FEAT])
        xc = sb("xc", [TILE, BLOCKS, FEAT])
        sq = sb("sq", [TILE, BLOCKS, FEAT])
        h = sb("h", [TILE, BLOCKS, FEAT])
        stat = sb("stat", [TILE, 4, BLOCKS])
        acc = sb("acc", [128, ACC])
        stack = sb("stack", [128, ACC])
        h1_t = sb("h1_t", [128, NODES])
        h_t = h1_t[0:FEAT, :]
        degree = sb("degree", [TILE, BLOCKS])
        inv = sb("inv", [TILE, BLOCKS])
        inv_deg = sb("inv_deg", [ROWS, NODES])
        gath = [sb(f"gath{s}", [TILE, GROUP, FEAT]) for s in range(2)]
        ef = [sb(f"ef{s}", [128, GEDGES]) for s in range(2)]
        hid = [sb(f"hid{s}", [128, GEDGES]) for s in range(2)]
        dprod = sb("dprod", [TILE, GROUP, 3, MUL])
        z_av = [sb(f"z_av{s}", [TILE, GROUP, FEAT]) for s in range(2)]
        z_sd = [sb(f"z_sd{s}", [TILE, GROUP, 2, MUL]) for s in range(2)]
        distance = [sb(f"distance{s}", [TILE, GROUP, WINDOW]) for s in range(2)]
        prod = sb("prod", [TILE, GROUP, PATHS, MUL, MUL])
        msg = [sb(f"msg{s}", [TILE, GROUP, ROWS]) for s in range(2)]
        hot = [sb(f"hot{s}", [TILE, GROUP, WINDOW]) for s in range(2)]

        src_f = sb("src_f", [TILE, TILES])
        src_p = sb("src_p", [TILE, TILES])
        src_b = sb("src_b", [TILE, TILES])
        key = sb("key", [TILE, TILES])
        pool_src = [sb(f"pool_src{s}", [TILE, GROUP], U32) for s in range(2)]
        pool_rows = [sb(f"pool_rows{s}", [TILE, GROUP, FEAT]) for s in range(2)]
        pool_hot = [sb(f"pool_hot{s}", [TILE, GROUP, WINDOW]) for s in range(2)]
        parts = sb("parts", [TILE, BLOCKS, 128], BF16)
        row_hot = sb("row_hot", [TILE, COUNTED_TILES, 128], BF16)
        column_hot = sb("column_hot", [TILE, COUNTED_TILES, COUNTS], BF16)
        counts = [sb(f"counts{c}", [128, COUNTS], F16) for c in range(len(COUNTED))]

        psum = ctx.enter_context(nc.psum_tensor("psum", [128, 8, BANK], F32))
        weights_ps = [psum[:TILE, 0:5, :].rearrange("p k n -> p (k n)")[:, s * GROUP * WCOLS:(s + 1) * GROUP * WCOLS]
                      .rearrange("p (t n) -> p t n", t=GROUP) for s in range(2)]
        SHARED = [GROUP - 1, 0]
        FIRST = (GROUP - 1) * TILE
        hid_ps = [(0, FIRST, psum[:HID0, 5, 0:FIRST]), (FIRST, GEDGES, psum[:HID0, 6, 0:TILE])]
        window_ps = psum[0:ROWS, 7, 0:WINDOW]
        counts_ps = [psum[:, 0:3, :], psum[:, 3:6, :], psum[:, 0:3, :]]
        counted_ps = psum[:, 6, 0:WINDOW]
        pooled_ps = psum[:FEAT, 7, 0:WINDOW]

        x_in_s = sem("x_in_s")
        groups_in = sem("groups_in")
        const_in_s = sem("const_in_s")
        graph_in = sem("graph_in")
        GRAPH_IN = 3 * 16
        par_in = sem("par_in")
        PAR_IN = 12 * 16
        filled = sem("filled")
        eps_ready = sem("eps_ready")
        si_zeroed = sem("si_zeroed")
        sage_filled = sem("sage_filled")
        src_step = sem("src_step")
        zeroed = sem("zeroed")
        span_ready = sem("span_ready")
        diag_ready = sem("diag_ready")
        diag_summed = sem("diag_summed")
        var_ready = [sem(f"var_ready{k}") for k in range(2)]
        std_ready = [sem(f"std_ready{k}") for k in range(2)]
        h_ready = [sem(f"h_ready{k}") for k in range(2)]
        table_in = [sem(f"table_in{ph}") for ph in range(3)]
        h_turned = [sem(f"h_turned{k}") for k in range(2)]
        h_t_ready = [sem(f"h_t_ready{k}") for k in range(2)]
        si_summed = sem("si_summed")
        sums_turned = [sem(f"sums_turned{k}") for k in range(2)]
        inv_ready = sem("inv_ready")
        inv_stored = sem("inv_stored")
        inv_deg_in = sem("inv_deg_in")
        mean_ready = sem("mean_ready")
        sage1_summed = sem("sage1_summed")
        h1_ready = sem("h1_ready")
        y_summed = sem("y_summed")
        y_ready = sem("y_ready")
        y_left = sem("y_left")
        out_ready = sem("out_ready")
        out_stored = sem("out_stored")
        step_dve = sem("step_dve")
        src_copied = sem("src_copied")
        gathered = [sem(f"gathered{s}") for s in range(2)]
        d_read = sem("d_read")
        d_ready = sem("d_ready")
        factors_ready = sem("factors_ready")
        away = sem("away")
        hot_ready = sem("hot_ready")
        summed = [sem(f"summed{ph}") for ph in range(3)]
        added = [sem(f"added{ph}") for ph in range(3)]
        pool_src_ready = [[sem(f"pool_src_ready{ph}{s}") for s in range(2)] for ph in (1, 2)]
        pool_in = [[sem(f"pool_in{ph}{s}") for s in range(2)] for ph in (1, 2)]
        parts_step = sem("parts_step")
        parts_ready = [sem(f"parts_ready{ph}") for ph in (1, 2)]
        key_step = [sem(f"key_step{ph}") for ph in (1, 2)]
        edges_hot = [sem(f"edges_hot{ph}") for ph in (1, 2)]
        tile_counted = [sem(f"tile_counted{ph}") for ph in (1, 2)]
        counts_ready = [sem(f"counts_ready{ph}") for ph in (1, 2)]
        far = [sem(f"far{ph}") for ph in (1, 2)]
        pool_hot_ready = [sem(f"pool_hot_ready{ph}") for ph in (1, 2)]
        base_ready = [sem(f"base_ready{ph}") for ph in range(3)]
        ef_in = [sem(f"ef_in{s}") for s in range(2)]
        hid_summed = sem("hid_summed")
        hid_ready = sem("hid_ready")
        weights_ready = sem("weights_ready")
        weights_read = sem("weights_read")
        products_summed = sem("products_summed")
        msg_ready = sem("msg_ready")

        def passes(eng):
            eng.wait_ge(span_ready, 1)
            more = eng.value_load(more_passes[0:1, 0:1], min_val=0, max_val=(NODES - 1) // WINDOW)
            return eng.snap(more + 1, min_val=1, max_val=(NODES - 1) // WINDOW + 1)

        def group_of(n0, u, i):
            return i, n0 + i, i % 2, u[i % 2] + i // 2, i >= 1, i >= 2

        def over_groups(eng, n_pass, lead, step, tail, begin=None):
            with eng.Fori(0, n_pass) as j:
                if begin is not None:
                    begin(j)
                n0 = eng.snap(j * GROUPS)
                u = [eng.snap(j * USES[s]) for s in range(2)]
                at = lambda i: (lambda k: group_of(n0, u, i + k) if 0 <= i + k < GROUPS else None)
                lead(at(0))
                for s in range(2):
                    step(at(s))
                with eng.Fori(1, BODIES) as b:
                    g = eng.snap(b * 2)
                    n = eng.snap(n0 + g)
                    for s in range(2):
                        step(lambda k, s=s: (g + (s + k), n + (s + k), (s + k) % 2, u[(s + k) % 2] + b + (s + k) // 2,
                                             2 + s + k >= 1, 2 + s + k >= 2))
                step(at(GROUPS - 1))
                tail(at(GROUPS), j)

        def nothing(group):
            pass

        def over_units(eng, n_pass, lead, unit, tail, begin=None):
            with eng.Fori(0, n_pass) as j:
                if begin is not None:
                    begin(j)
                n0 = eng.snap(j * ALL_UNITS)
                lead(n0)
                unit(0, n0, 0, False)
                unit(1, eng.snap(n0 + 1), 1, False)
                with eng.Fori(2, ALL_UNITS - 1) as u:
                    unit(u, eng.snap(n0 + u), 2, False)
                unit(ALL_UNITS - 1, eng.snap(n0 + (ALL_UNITS - 1)), 2, True)
                tail(j, eng.snap(n0 + ALL_UNITS))

        def turn(n, q):
            return n * UNIT + (q + 1)

        def copied(n, c):
            return n * (2 * len(COUNTED)) + (2 * c + 2)

        def of_block(t, b):
            return t[:, b:b + (TILE - 1) * BLOCKS + 1:BLOCKS]

        block = ctx.enter_context(nc.Block())

        @block.sync
        def _(sp):
            sp.dma_start(x[:, :, :], x_in.rearrange("(p b) f -> p b f", b=BLOCKS)).then_inc(x_in_s, 16)
            sp.dma_start(dstg_raw[:, :], dst_groups_in).then_inc(groups_in, 16)
            sp.dma_start(const[:, :], const_in).then_inc(const_in_s, 16)
            sp.dma_start(src_all[:, :], src_in.bitcast(U32)).then_inc(graph_in, 16)
            sp.dma_start(dst_raw[:, :], dst_tiles_in).then_inc(graph_in, 16)
            sp.dma_start(sh_all[:, :, :], sh_in).then_inc(graph_in, 16)
            sp.wait_ge(si_zeroed, 1)
            sp.dma_start(si[0:MUL, 0:MUL], si0_in).then_inc(par_in, 16)
            for m in range(3):
                sp.dma_start(si[MUL * (m + 1):MUL * (m + 2), MUL + m:MUL + m + 3 * MUL - 2:3], si1_in,
                             allow_slow_non_contiguous=True).then_inc(par_in, 16)
            sp.dma_start(columns[:, :], columns_in.broadcast_to([128, COUNTS])).then_inc(par_in, 16)
            n_pass = passes(sp)
            sp.wait_ge(zeroed, 1)

            def load_edges(group):
                i, n, s, use, _, third = group(0)
                if third:
                    sp.wait_ge(hid_summed, n - 1)
                sp.dma_start(ef[s][0:FEAT, :], ef_t_in[:, bass.ds(i * GEDGES, GEDGES)]).then_inc(ef_in[s], 16)

            def end(group, j):
                sp.wait_ge(added[0], (j + 1) * GROUPS)

            over_groups(sp, n_pass, nothing, load_edges, end)
            sp.wait_ge(inv_ready, 1)
            sp.dma_start(inv_row.rearrange("o (p b) -> (o p) b", b=BLOCKS), inv[:, :]).then_inc(inv_stored, 16)
            sp.wait_ge(inv_stored, 16)
            sp.wait_ge(table_in[1], 16)
            sp.dma_start(inv_deg[:, :], inv_row.broadcast_to([ROWS, NODES])).then_inc(inv_deg_in, 16)
            sp.wait_ge(out_stored, 16)

        @block.gpsimd
        def _(pool):
            gps = nc.gpsimd
            gps.memset(eps[:, :], EPS).then_inc(eps_ready, 1)
            gps.memset(si[:, :], 0.0).then_inc(si_zeroed, 1)
            gps.memset(ones[:, :], 1.0)
            gps.memset(w1[:, :], 0.0)
            gps.memset(ef[0][:, :], 0.0)
            gps.memset(ef[1][:, :], 0.0)
            gps.memset(sage2[:, :], 0.0)
            gps.memset(w2[:, :], 0.0).then_inc(zeroed, 1)
            gps.memset(h1_t[:, :], 0.0)
            for s in range(2):
                gps.memset(msg[s][:, :, DEG:ROWS], 1.0)
                gps.memset(hid[s][:, :], 1.0)
            gps.memset(acc[:, :], 0.0).then_inc(filled, 1)
            gps.memset(stack[:, :], 0.0)
            gps.memset(parts[:, :, ROWS:128], 0.0)
            gps.memset(row_hot[:, :, TILE:128], 0.0).then_inc(sage_filled, 1)
            n_pass = passes(pool)

            def gather(group):
                i, n, s, use, _, third = group(0)
                pool.wait_ge(src_copied, n + 1)
                if third:
                    pool.wait_ge(d_read, n - 1)
                    pool.wait_ge(factors_ready, n - 1)
                pool.wait_ge(table_in[0], 16)
                pool.nop(nofuse=True)
                for t in range(GROUP):
                    pool.indirect_dma_start(
                        out=gath[s][:, t, :], out_offset=None, in_=tables[0],
                        in_offset=bass.IndirectOffsetOnAxis(ap=src_slot[s][:, t:t + 1], axis=0),
                    ).then_inc(gathered[s], 16)

            def end(group, j):
                pool.wait_ge(added[0], (j + 1) * GROUPS)

            over_groups(pool, n_pass, nothing, gather, end)

            for ph in (1, 2):
                high, mid, low = (parts[:, :, k * FEAT:(k + 1) * FEAT] for k in range(PARTS))
                pool.wait_ge(h_ready[1] if ph == 1 else y_ready, 1)
                gps.tensor_copy(high, h[:, :, :]).then_inc(parts_step, 1)
                pool.wait_ge(parts_step, (ph - 1) * 3 + 1)
                gps.tensor_tensor(xc[:, :, :], h[:, :, :], high, ALU.subtract).then_inc(parts_step, 1)
                pool.wait_ge(parts_step, (ph - 1) * 3 + 2)
                gps.tensor_copy(mid, xc[:, :, :]).then_inc(parts_step, 1)
                pool.wait_ge(parts_step, (ph - 1) * 3 + 3)
                gps.tensor_tensor(low, xc[:, :, :], mid, ALU.subtract).then_inc(parts_ready[ph - 1], 1)

                def unit(u, n, k, last, ph=ph):
                    for s, q in enumerate(POOLED):
                        pool.wait_ge(pool_src_ready[ph - 1][s], n + 1)
                        if k:
                            pool.wait_ge(summed[ph], turn(n - 1, q))
                        pool.wait_ge(table_in[ph], 16)
                        pool.nop(nofuse=True)
                        for t in range(GROUP):
                            pool.indirect_dma_start(
                                out=pool_rows[s][:, t, :], out_offset=None, in_=tables[ph],
                                in_offset=bass.IndirectOffsetOnAxis(ap=pool_src[s][:, t:t + 1], axis=0),
                            ).then_inc(pool_in[ph - 1][s], 16)

                def end(j, n, ph=ph):
                    pool.wait_ge(added[ph], n * UNIT)

                over_units(pool, n_pass, nothing, unit, end)

        @block.scalar
        def _(act):
            act.wait_ge(eps_ready, 1)
            nc.scalar.activation(eps_root[:, :], eps[:, :], ACT.Sqrt)
            act.wait_ge(zeroed, 1)
            act.dma_start(w1[0:FEAT, :], w1_in).then_inc(par_in, 16)
            act.dma_start(b1[:, :], b1_in).then_inc(par_in, 16)
            act.dma_start(w2[0:HID0 + 1, :], w2_in).then_inc(par_in, 16)
            act.dma_start(sage1[:, :], sage1_in).then_inc(par_in, 16)
            act.dma_start(sage1_b[:, :], sage1_b_in).then_inc(par_in, 16)
            act.dma_start(sage2[0:HID1, 0:2 * FEAT], sage2_in).then_inc(par_in, 16)
            act.dma_start(sage2_b[:, :], sage2_b_in.broadcast_to([TILE, FEAT])).then_inc(par_in, 16)

            def std_and_table(k):
                act.wait_ge(var_ready[k], 1)
                nc.scalar.activation(stat[:, 2, :], stat[:, 1, :], ACT.Sqrt, bias=eps[:TILE, :],
                                     scale=1.0 / FEAT).then_inc(std_ready[k], 1)
                act.wait_ge(h_ready[k], 1)
                act.dma_start(tables[k].rearrange("(p b) f -> p b f", b=BLOCKS), h[:, :, :]).then_inc(table_in[k], 16)
                if k == 0:
                    act.wait_ge(filled, 1)
                to = (h_t if k == 0 else stack[ROWS:128, 0:NODES]).rearrange("f (p b) -> f b p", b=BLOCKS)
                for c in range(0, BLOCKS, 4):
                    w = min(4, BLOCKS - c)
                    act.wait_ge(h_turned[k], c // 4 + 1)
                    last = nc.scalar.copy(to[:, c:c + w, :],
                                          psum[:FEAT, c // 4, 0:w * TILE].rearrange("f (b p) -> f b p", b=w))
                last.then_inc(h_t_ready[k], 1)

            std_and_table(0)
            n_pass = passes(act)
            act.wait_ge(par_in, PAR_IN)
            act.wait_ge(graph_in, GRAPH_IN)

            def copy_src(group):
                i, n, s, use, _, third = group
                if third:
                    act.wait_ge(gathered[s], use * (16 * GROUP))
                nc.scalar.copy(src_slot[s][:, :], src_all[:, bass.ds(i * GROUP, GROUP)]).then_inc(src_copied, 1)

            def relu(group):
                i, n, s, use, _, third = group
                act.wait_ge(hid_summed, n + 1)
                if third:
                    act.wait_ge(weights_ready, n - 1)
                for a, z, ps in hid_ps:
                    last = nc.scalar.activation(hid[s][0:HID0, a:z], ps, ACT.Relu, bias=b1[:, 0:1])
                last.then_inc(hid_ready, 1)

            def distances(to, i):
                for t in range(GROUP):
                    last = nc.scalar.activation(to[:, t, :], iota[:TILE, :], ACT.Abs,
                                                bias=dst_rel[:, bass.ds(i * GROUP + t, 1)])
                return last

            def one_hot(to, of):
                return nc.scalar.activation(to, of, ACT.Relu, bias=1.0, scale=-1.0)

            def group_one_hot(group):
                i, n, s, use, _, third = group
                if third:
                    act.wait_ge(hot_ready, n - 1)
                distances(distance[s], i).then_inc(away, 1)
                if third:
                    act.wait_ge(summed[0], n - 1)
                act.wait_ge(away, n + 1)
                one_hot(hot[s][:, :, :], distance[s][:, :, :]).then_inc(hot_ready, 1)

            def factors(group):
                i, n, s, use, _, third = group
                act.wait_ge(gathered[s], (use + 1) * (16 * GROUP))
                if third:
                    act.wait_ge(weights_read, n - 1)
                for t in range(GROUP):
                    nc.scalar.activation(z_av[s][:, t, :], gath[s][:, t, :], ACT.Copy,
                                         scale=sh_all[:, bass.ds(i * GROUP + t, 1), 0])
                nc.scalar.copy(z_sd[s][:, :, 0, :], gath[s][:, :, 0:MUL]).then_inc(factors_ready, 1)

            def ahead(group):
                relu(group(0))
                if group(-1) is not None:
                    factors(group(-1))
                    if group(1) is not None:
                        copy_src(group(1))
                    group_one_hot(group(-1))

            def lead(group):
                copy_src(group(0))
                copy_src(group(1))

            def begin(j):
                act.wait_ge(base_ready[0], j * 2 + 1)

            def end(group, j):
                factors(group(-1))
                group_one_hot(group(-1))
                act.wait_ge(added[0], (j + 1) * GROUPS)

            over_groups(act, n_pass, lead, ahead, end, begin)
            std_and_table(1)

            for ph in (1, 2):
                def copy_pool_src(u, n, s, k, ph=ph):
                    if k:
                        act.wait_ge(pool_in[ph - 1][s], n * (16 * GROUP))
                    nc.scalar.copy(pool_src[s][:, :], src_all[:, bass.ds((u * UNIT + POOLED[s]) * GROUP, GROUP)]
                                   ).then_inc(pool_src_ready[ph - 1][s], 1)

                def pool_one_hot(u, n, s, k, ph=ph):
                    if k:
                        act.wait_ge(pool_hot_ready[ph - 1], n * 2 + (s - 1))
                    distances(distance[s], u * UNIT + POOLED[s]).then_inc(far[ph - 1], 1)
                    if k:
                        act.wait_ge(summed[ph], turn(n - 1, POOLED[s]))
                    act.wait_ge(far[ph - 1], n * 2 + (s + 1))
                    one_hot(pool_hot[s][:, :, :], distance[s][:, :, :]).then_inc(pool_hot_ready[ph - 1], 1)

                def copy_counts(n, c, k, ph=ph):
                    act.wait_ge(tile_counted[ph - 1], n * COUNTED_TILES + (c + 1) * GROUP)
                    if k:
                        act.wait_ge(summed[ph], turn(n - 1, COUNTED[c]))
                    first, rest = COUNT_CUTS[1], COUNT_CUTS[2] - COUNT_CUTS[1]
                    nc.scalar.copy(counts[c][:, 0:first], counts_ps[c][:, 0, 0:first]
                                   ).then_inc(counts_ready[ph - 1], 1)
                    nc.scalar.copy(counts[c][:, first:].rearrange("p (k n) -> p k n", n=rest),
                                   counts_ps[c][:, 1:, 0:rest]).then_inc(counts_ready[ph - 1], 1)

                def unit(u, n, k, last):
                    copy_counts(n, 0, k)
                    copy_pool_src(u, n, 1, k)
                    pool_one_hot(u, n, 0, k)
                    copy_counts(n, 1, k)
                    if not last:
                        copy_pool_src(u + 1, n + 1, 0, 1)
                    copy_counts(n, 2, k)
                    pool_one_hot(u, n, 1, k)

                def begin(j, ph=ph):
                    act.wait_ge(base_ready[ph], j * 2 + 1)

                def lead(n):
                    copy_pool_src(0, n, 0, 0)

                def end(j, n, ph=ph):
                    act.wait_ge(added[ph], n * UNIT)

                over_units(act, n_pass, lead, unit, end, begin)
                if ph == 1:
                    for k, a in enumerate(range(0, NODES, CHUNK)):
                        w = min(CHUNK, NODES - a)
                        act.wait_ge(sage1_summed, k + 1)
                        last = nc.scalar.activation(h1_t[0:HID1, a:a + w], psum[:HID1, k, 0:w], ACT.Relu,
                                                    bias=sage1_b[:, 0:1])
                    last.then_inc(h1_ready, 1)
                    act.wait_ge(y_ready, 1)
                    act.dma_start(tables[2].rearrange("(p b) f -> p b f", b=BLOCKS), h[:, :, :]
                                  ).then_inc(table_in[2], 16)
            act.wait_ge(out_ready, 1)
            act.dma_start(out.rearrange("(p b) f -> p b f", b=BLOCKS), h[:, :, :]).then_inc(out_stored, 16)

        @block.tensor
        def _(pe):
            pe.wait_ge(zeroed, 1)
            pe.wait_ge(diag_ready, 1)
            nc.tensor.matmul(psum[:, 7, 0:2 * GROUPS], ones[0:GROUPS, :], diag[:, :, :], start=True,
                             stop=True).then_inc(diag_summed, 1)

            def turn_h(k):
                pe.wait_ge(h_ready[k], 1)
                for b in range(BLOCKS):
                    last = nc.tensor.transpose(psum[:FEAT, b // 4, (b % 4) * TILE:(b % 4 + 1) * TILE], h[:, b, :],
                                               ident[:TILE, :TILE])
                    if b % 4 == 3 or b == BLOCKS - 1:
                        last.then_inc(h_turned[k], 1)

            def turn_sums(k):
                for b in range(BLOCKS):
                    at = b % TURNED * ROWS
                    last = nc.tensor.transpose(psum[:TILE, b // TURNED, at:at + ROWS], of_block(acc[0:ROWS, :], b),
                                               ident[:ROWS, :ROWS])
                    if b % TURNED == TURNED - 1:
                        last.then_inc(sums_turned[k], 1)

            turn_h(0)
            n_pass = passes(pe)
            pe.wait_ge(par_in, PAR_IN)
            pe.wait_ge(filled, 1)
            pe.wait_ge(h_t_ready[0], 1)
            for ph in range(3):
                def hidden(group):
                    i, n, s, use, second, third = group
                    pe.wait_ge(ef_in[s], (use + 1) * 16)
                    if second:
                        pe.wait_ge(hid_ready, n)
                    for a, z, ps in hid_ps:
                        last = nc.tensor.matmul(ps, w1[:, :], ef[s][:, a:z], start=True, stop=True)
                    last.then_inc(hid_summed, 1)

                def weights(group):
                    i, n, s, use, second, third = group
                    pe.wait_ge(hid_ready, n + 1)
                    if third:
                        pe.wait_ge(weights_read, n - 1)
                    for t in sorted(range(GROUP), key=lambda t: t == SHARED[s]):
                        if t == SHARED[s] and second:
                            pe.wait_ge(weights_read, n)
                        last = nc.tensor.matmul(weights_ps[s][:, t, :], hid[s][:, t * TILE:(t + 1) * TILE], w2[:, :],
                                                start=True, stop=True)
                    last.then_inc(weights_ready, 1)

                def window(group):
                    i, n, s, use, second, third = group
                    pe.wait_ge(msg_ready, n + 1)
                    pe.wait_ge(hot_ready, n + 1)
                    if second:
                        pe.wait_ge(added[0], n)
                    for t in range(GROUP):
                        last = nc.tensor.matmul(window_ps, msg[s][:, t, :], hot[s][:, t, :],
                                                start=(t == 0), stop=(t == GROUP - 1))
                    last.then_inc(summed[0], 1)

                def end(group, j, ph=ph):
                    pe.wait_ge(added[ph], (j + 1) * GROUPS)

                if ph == 0:
                    def ahead(group):
                        if group(2) is not None:
                            hidden(group(2))
                        if group(1) is not None:
                            weights(group(1))
                        window(group(0))

                    def lead(group):
                        hidden(group(0))
                        hidden(group(1))
                        weights(group(0))

                    def self_interaction(a, z):
                        for b in range(a, z):
                            last = nc.tensor.matmul(psum[:TILE, 5 + b // 16, (b % 16) * FEAT:(b % 16 + 1) * FEAT],
                                                    of_block(h_t, b), si[0:FEAT, :], start=True, stop=True)
                        if z == BLOCKS:
                            last.then_inc(si_summed, 1)

                    with pe.Fori(0, n_pass) as j:
                        n0 = pe.snap(j * GROUPS)
                        u = [pe.snap(j * USES[s]) for s in range(2)]
                        at = lambda i: (lambda k: group_of(n0, u, i + k) if 0 <= i + k < GROUPS else None)
                        lead(at(0))
                        ahead(at(0))
                        with pe.Fori(1, BODIES) as b:
                            n = pe.snap(n0 + b * 2)
                            for s in (-1, 0):
                                ahead(lambda k, s=s: (None, n + (s + k), (s + k) % 2,
                                                      u[(s + k) % 2] + b + (s + k) // 2,
                                                      2 + s + k >= 1, 2 + s + k >= 2))
                        weights(at(GROUPS - 2)(1))
                        self_interaction(0, 16)
                        window(at(GROUPS - 2)(0))
                        self_interaction(16, BLOCKS)
                        window(at(GROUPS - 1)(0))
                        end(None, j)
                    turn_sums(0)
                    turn_h(1)
                    pe.wait_ge(h_t_ready[1], 1)
                else:
                    def count_group(n, c, k, ph=ph):
                        before = {0: -1, 1: -2, 2: 0}[c]
                        for t in range(GROUP):
                            e = c * GROUP + t
                            pe.wait_ge(edges_hot[ph - 1], n * COUNTED_TILES + (e + 1))
                            for i, (a, z) in enumerate(zip(COUNT_CUTS, COUNT_CUTS[1:])):
                                if t == 0 and i < 2 and (c == 2 or k):
                                    pe.wait_ge(counts_ready[ph - 1], copied(n, before) - 1 + i)
                                last = nc.tensor.matmul(counts_ps[c][:, i, 0:z - a], row_hot[:, e, :],
                                                        column_hot[:, e, a:z], start=(t == 0), stop=(t == GROUP - 1))
                            last.then_inc(tile_counted[ph - 1], 1)

                    def counted_window(n, c, first, ph=ph):
                        pe.wait_ge(counts_ready[ph - 1], copied(n, c))
                        if not first:
                            pe.wait_ge(added[ph], turn(n, COUNTED[c - 1]) if c else turn(n - 1, COUNTED[2]))
                        for b in range(BLOCKS):
                            last = nc.tensor.matmul(counted_ps, parts[:, b, :],
                                                    counts[c][:TILE, b * WINDOW:(b + 1) * WINDOW],
                                                    start=(b == 0), stop=(b == BLOCKS - 1))
                        last.then_inc(summed[ph], 1)

                    def pooled_window(n, s, first, ph=ph):
                        pe.wait_ge(pool_hot_ready[ph - 1], n * 2 + (s + 1))
                        pe.wait_ge(pool_in[ph - 1][s], (n + 1) * (16 * GROUP))
                        if not first:
                            pe.wait_ge(added[ph], turn(n, POOLED[0]) if s else turn(n - 1, POOLED[1]))
                        for t in range(GROUP):
                            last = nc.tensor.matmul(pooled_ps, pool_rows[s][:, t, :], pool_hot[s][:, t, :],
                                                    start=(t == 0), stop=(t == GROUP - 1))
                        last.then_inc(summed[ph], 1)

                    def unit(u, n, k, last):
                        count_group(n, 0, k)
                        if k:
                            counted_window(n - 1, 2, False)
                            pooled_window(n - 1, 1, False)
                        count_group(n, 1, k)
                        counted_window(n, 0, not k)
                        count_group(n, 2, k)
                        counted_window(n, 1, False)
                        pooled_window(n, 0, not k)

                    def unit_end(j, n, ph=ph):
                        counted_window(n - 1, 2, False)
                        pooled_window(n - 1, 1, False)
                        pe.wait_ge(added[ph], n * UNIT)

                    pe.wait_ge(parts_ready[ph - 1], 1)
                    over_units(pe, n_pass, nothing, unit, unit_end)
                    if ph == 1:
                        for k, a in enumerate(range(0, NODES, CHUNK)):
                            w = min(CHUNK, NODES - a)
                            pe.wait_ge(mean_ready, k + 1)
                            nc.tensor.matmul(psum[:HID1, k, 0:w], sage1[:, :], stack[:, a:a + w], start=True,
                                             stop=True).then_inc(sage1_summed, 1)
                        pe.wait_ge(h1_ready, 1)
                        for b in range(BLOCKS):
                            last = nc.tensor.matmul(psum[:TILE, b // 4, (b % 4) * 128:(b % 4 + 1) * 128],
                                                    of_block(h1_t, b), sage2[:, :], start=True, stop=True)
                            if b % 4 == 3 or b == BLOCKS - 1:
                                last.then_inc(y_summed, 1)
                        pe.wait_ge(y_left, 1)
                    else:
                        turn_sums(1)

        @block.vector
        def _(dve):
            vec = nc.vector
            steps = [0]

            def done(ins):
                steps[0] += 1
                ins.then_inc(step_dve, 1)
                dve.wait_ge(step_dve, steps[0])

            dve.wait_ge(const_in_s, 16)
            dve.wait_ge(groups_in, 16)
            done(vec.tensor_copy(dstg_f[:, :], dstg_raw[:, :]))
            vec.tensor_reduce(low_high[:, 0:1], dstg_f[:, :], AX_X, ALU.min)
            done(vec.tensor_reduce(low_high[:, 1:2], dstg_f[:, :], AX_X, ALU.max))
            done(vec.tensor_tensor(low_high[:, 2:3], low_high[:, 1:2], low_high[:, 0:1], ALU.subtract))
            vec.tensor_scalar(diag[:, 0, :], ident[:GROUPS, :GROUPS], low_high[:, 0:1], None, ALU.mult)
            vec.tensor_scalar(diag[:, 1, :], ident[:GROUPS, :GROUPS], low_high[:, 2:3], None,
                              ALU.mult).then_inc(diag_ready, 1)
            def layernorm_relu(k):
                done(vec.tensor_reduce(stat[:, 0, :], x[:, :, :], AX_X, ALU.add))
                done(vec.tensor_scalar(stat[:, 0, :], stat[:, 0, :], 1.0 / FEAT, None, ALU.mult))
                done(vec.tensor_tensor(xc[:, :, :], x[:, :, :], spread(stat[:, 0, :], FEAT), ALU.subtract))
                done(vec.tensor_tensor(sq[:, :, :], xc[:, :, :], xc[:, :, :], ALU.mult))
                vec.tensor_reduce(stat[:, 1, :], sq[:, :, :], AX_X, ALU.add).then_inc(var_ready[k], 1)
                dve.wait_ge(std_ready[k], 1)
                done(vec.reciprocal(stat[:, 3, :], stat[:, 2, :]))
                done(vec.tensor_tensor(xc[:, :, :], xc[:, :, :], spread(stat[:, 3, :], FEAT), ALU.mult))
                if k == 0:
                    vec.tensor_scalar(h[:, :, 0:MUL], xc[:, :, 0:MUL], 0.0, None, ALU.max)
                    vec.tensor_scalar(h[:, :, MUL:FEAT].rearrange("p b (m i) -> p b m i", m=3),
                                      xc[:, :, MUL:FEAT].rearrange("p b (i m) -> p b m i", m=3), 0.0, None,
                                      ALU.max).then_inc(h_ready[k], 1)
                else:
                    vec.tensor_scalar(h[:, :, :], xc[:, :, :], 0.0, None, ALU.max).then_inc(h_ready[k], 1)

            def spread(a, n):
                return a.unsqueeze(2).to_broadcast([a.shape[0], a.shape[1], n])

            dve.wait_ge(x_in_s, 16)
            layernorm_relu(0)
            dve.wait_ge(diag_summed, 1)
            done(vec.tensor_copy(base0[:, :, :], psum[:, 7, 0:2 * GROUPS].rearrange("p (k g) -> p k g", k=2)))
            done(vec.tensor_reduce(span_f[:, :], base0[0:1, 1, :], AX_X, ALU.max))
            done(vec.tensor_scalar(span_f[:, :], span_f[:, :], 1.0 / WINDOW, 0.5 / WINDOW - 0.5, ALU.mult, ALU.add))
            done(vec.tensor_scalar(span_f[:, :], span_f[:, :], ROUND, None, ALU.add))
            done(vec.tensor_scalar(span_f[:, :], span_f[:, :], ROUND, None, ALU.subtract))
            vec.tensor_copy(more_passes[:, :], span_f[:, :]).then_inc(span_ready, 1)
            dve.wait_ge(graph_in, GRAPH_IN)
            vec.tensor_copy(dst_f[:, :], dst_raw[:, :])
            done(vec.tensor_scalar(sh_all[:, :, :], sh_all[:, :, :], ALPHA, None, ALU.mult))
            vec.tensor_scalar(shc_all[:, :, :], sh_all[:, :, 1:4], float(C110), None, ALU.mult)
            dve.wait_ge(par_in, PAR_IN)
            done(vec.tensor_scalar(si[:, :], si[:, :], float(SI_SCALE), None, ALU.mult))

            dve.wait_ge(filled, 1)
            n_pass = passes(dve)

            def place_windows(ph, j):
                vec.tensor_tensor(dst_rel[:, :].rearrange("p (g t) -> p g t", t=GROUP), spread(base[:TILE, :], GROUP),
                                  dst_f[:, :].rearrange("p (g t) -> p g t", t=GROUP), ALU.subtract)
                vec.tensor_copy(base_row[:, :], base[0:1, :]).then_inc(base_ready[ph], 1)
                dve.wait_ge(base_ready[ph], j * 2 + 1)

            def move_windows(ph, j):
                dve.wait_ge(added[ph], (j + 1) * GROUPS)
                vec.tensor_scalar(base[:, :], base[:, :], float(WINDOW), float(NODES), ALU.add,
                                  ALU.min).then_inc(base_ready[ph], 1)
                dve.wait_ge(base_ready[ph], j * 2 + 2)

            def add_window(group, behind=False):
                i, n, s, use, _, _ = group
                at = dve.value_load(base_row[0:1, bass.ds(i, 1)], min_val=0, max_val=NODES)
                dve.wait_ge(summed[0], n + 1)
                if behind:
                    dve.wait_ge(added[0], n)
                to = acc[0:ROWS, bass.ds(at, WINDOW)]
                vec.tensor_tensor(to, to, window_ps, ALU.add).then_inc(added[0], 1)

            def factor_d(group):
                i, n, s, use, _, _ = group
                shc = shc_all[:, bass.ds(i * GROUP, GROUP), :]
                dve.wait_ge(gathered[s], (use + 1) * (16 * GROUP))
                vec.tensor_tensor(dprod[:, :, :, :], gath[s][:, :, MUL:FEAT].rearrange("p t (m i) -> p t m i", m=3),
                                  shc.unsqueeze(3).to_broadcast([TILE, GROUP, 3, MUL]), ALU.mult).then_inc(d_read, 1)

            def sum_factor_d(group):
                i, n, s, use, _, _ = group
                dve.wait_ge(d_read, n + 1)
                vec.tensor_reduce(z_sd[s][:, :, 1, :], dprod[:, :, :, :].rearrange("p t m i -> p t i m"), AX_X,
                                  ALU.add).then_inc(d_ready, 1)

            def products(group):
                i, n, s, use, _, _ = group
                w = weights_ps[s]
                dve.wait_ge(d_ready, n + 1)
                dve.wait_ge(factors_ready, n + 1)
                dve.wait_ge(weights_ready, n + 1)
                vec.tensor_tensor(prod[:, :, 0, :, :], w[:, :, 0:64].rearrange("p t (i o) -> p t i o", i=MUL),
                                  z_av[s][:, :, 0:MUL].unsqueeze(3).to_broadcast([TILE, GROUP, MUL, MUL]), ALU.mult)
                vec.tensor_tensor(
                    prod[:, :, 1:4, :, :].rearrange("p t m i o -> p t (m i) o"),
                    w[:, :, 64:128].rearrange("p t (m n) -> p t m n", m=1).to_broadcast([TILE, GROUP, 3, 64]),
                    z_av[s][:, :, MUL:FEAT].unsqueeze(3).to_broadcast([TILE, GROUP, 3 * MUL, MUL]), ALU.mult)
                vec.tensor_tensor(prod[:, :, 4:6, :, :].rearrange("p t c i o -> p t (c i) o"),
                                  w[:, :, 128:256].rearrange("p t (i o) -> p t i o", o=MUL),
                                  z_sd[s][:, :, :, :].rearrange("p t c i -> p t (c i)").unsqueeze(3)
                                  .to_broadcast([TILE, GROUP, 2 * MUL, MUL]), ALU.mult).then_inc(weights_read, 1)

            def sum_products(group):
                i, n, s, use, _, third = group
                if third:
                    dve.wait_ge(summed[0], n - 1)
                dve.wait_ge(weights_read, n + 1)
                vec.tensor_reduce(msg[s][:, :, 0:SUMS].rearrange("p t (c o) -> p t c o", c=PATHS),
                                  prod[:, :, :, :, :].rearrange("p t c i o -> p t c o i"), AX_X,
                                  ALU.add).then_inc(products_summed, 1)

            def times_sh1(group):
                i, n, s, use, _, _ = group
                dve.wait_ge(products_summed, n + 1)
                vec.tensor_tensor(msg[s][:, :, SUMS:SH_SUMS].rearrange("p t (m o) -> p t m o", m=3),
                                  msg[s][:, :, 4 * MUL:5 * MUL].unsqueeze(2).to_broadcast([TILE, GROUP, 3, MUL]),
                                  sh_all[:, bass.ds(i * GROUP, GROUP), 1:4].unsqueeze(3)
                                  .to_broadcast([TILE, GROUP, 3, MUL]), ALU.mult).then_inc(msg_ready, 1)

            def messages(group):
                sum_factor_d(group(0))
                if group(-2) is not None:
                    add_window(group(-2))
                if group(-1) is not None:
                    times_sh1(group(-1))
                products(group(0))
                if group(1) is not None:
                    factor_d(group(1))
                sum_products(group(0))

            for ph in range(3):
                sums = stack if ph == 1 else acc
                done(vec.tensor_copy(base[:, :], base0[:, 0, :]))
                if ph == 0:
                    def begin(j):
                        place_windows(0, j)

                        def src_done(ins, k):
                            ins.then_inc(src_step, 1)
                            dve.wait_ge(src_step, j * 7 + k)

                        src_done(vec.tensor_copy(src_f[:, :], src_all[:, :].bitcast(I32)), 1)
                        src_done(vec.tensor_scalar(src_p[:, :], src_f[:, :], 1.0 / BLOCKS, 0.5 / BLOCKS - 0.5,
                                                   ALU.mult, ALU.add), 2)
                        src_done(vec.tensor_scalar(src_p[:, :], src_p[:, :], ROUND, None, ALU.add), 3)
                        src_done(vec.tensor_scalar(src_p[:, :], src_p[:, :], ROUND - 1.0, None, ALU.subtract), 4)
                        src_done(vec.tensor_scalar(src_b[:, :], src_p[:, :], -float(BLOCKS), float(BLOCKS), ALU.mult,
                                                   ALU.add), 5)
                        src_done(vec.tensor_tensor(src_b[:, :], src_f[:, :], src_b[:, :], ALU.add), 6)
                        src_done(vec.tensor_scalar(src_b[:, :], src_b[:, :], float(WINDOW), 1.0, ALU.mult, ALU.add), 7)

                    def lead(group):
                        factor_d(group(0))

                    def end(group, j):
                        add_window(group(-2))
                        times_sh1(group(-1))
                        add_window(group(-1), behind=True)
                        dve.wait_ge(si_summed, j + 1)
                        move_windows(0, j)

                    over_groups(dve, n_pass, lead, messages, end, begin)
                    dve.wait_ge(sage_filled, 1)
                    for k, (a, z) in enumerate(((0, 16), (16, BLOCKS))):
                        last = vec.tensor_tensor(x[:, a:z, :], x[:, a:z, :], psum[:TILE, 5 + k, 0:(z - a) * FEAT]
                                                 .rearrange("p (b f) -> p b f", f=FEAT), ALU.add)
                    done(last)
                    for k in range(BLOCKS // TURNED):
                        a, z = k * TURNED, (k + 1) * TURNED
                        dve.wait_ge(sums_turned[0], k + 1)
                        got = psum[:TILE, k, 0:TURNED * ROWS].rearrange("p (b r) -> p b r", r=ROWS)
                        scalars = x[:, a:z, 0:MUL]
                        vectors = x[:, a:z, MUL:FEAT].rearrange("p b (o m) -> p b m o", m=3)
                        for s_row, v_row in ((0, MUL), (5 * MUL, SUMS)):
                            vec.tensor_tensor(scalars, scalars, got[:, :, s_row:s_row + MUL], ALU.add)
                            done(vec.tensor_tensor(vectors, vectors, got[:, :, v_row:v_row + 3 * MUL]
                                                   .rearrange("p b (m o) -> p b m o", m=3), ALU.add))
                        vec.tensor_scalar(degree[:, a:z], got[:, :, DEG], 1.0, None, ALU.max)
                    layernorm_relu(1)
                    vec.reciprocal(inv[:, :], degree[:, :]).then_inc(inv_ready, 1)
                else:
                    def load_bases(i, count):
                        _, at = nc.values_load_multi_w_load_instructions(
                            base_row[0:1, bass.ds(i, count)], engines=(mybir.EngineType.DVE,), min_val=0, max_val=NODES)
                        return at

                    def add_unit_window(at, q, done, first=False, ph=ph, sums=sums):
                        dve.wait_ge(summed[ph], done + 1)
                        if not first:
                            dve.wait_ge(added[ph], done)
                        to, window = (sums[0:FEAT, bass.ds(at, WINDOW)], pooled_ps) if q in POOLED else (
                            sums[0:ROWS, bass.ds(at, WINDOW)], counted_ps[0:ROWS, :])
                        vec.tensor_tensor(to, to, window, ALU.add).then_inc(added[ph], 1)

                    LATE = {0: 1, 1: 2, 5: 3, 6: 4}

                    def unit(u, n, k, last, ph=ph):
                        first_tile = u * (UNIT * GROUP) if isinstance(u, int) else dve.snap(u * (UNIT * GROUP))
                        counted = dve.snap(n * COUNTED_TILES)
                        group = u * UNIT if isinstance(u, int) else dve.snap(u * UNIT)
                        done_before = dve.snap(n * UNIT)
                        if k == 2:
                            at = load_bases(group - (2 * UNIT - 1), UNIT)
                        elif k == 1:
                            at = [None] * (UNIT - 1) + list(load_bases(0, 1))
                        for e in range(COUNTED_TILES):
                            if k:
                                dve.wait_ge(tile_counted[ph - 1], counted + (e + 1 - COUNTED_TILES))
                            tile = first_tile + (COUNTED[e // GROUP] * GROUP + e % GROUP)
                            vec.tensor_scalar(row_hot[:, e, 0:TILE], columns[:TILE, 0:TILE],
                                              src_p[:, bass.ds(tile, 1)], None, ALU.is_equal)
                            vec.tensor_scalar(column_hot[:, e, :], columns[:TILE, :],
                                              key[:, bass.ds(tile, 1)], None, ALU.is_equal
                                              ).then_inc(edges_hot[ph - 1], 1)
                            if e in LATE and k == 2:
                                q = LATE[e]
                                add_unit_window(at[q - 1], q, done_before + (q - 2 * UNIT))
                            if e == 10 and k:
                                add_unit_window(at[UNIT - 1], 0, done_before - UNIT, first=(k == 1))

                    def begin(j, ph=ph):
                        place_windows(ph, j)

                        def key_done(ins, k):
                            ins.then_inc(key_step[ph - 1], 1)
                            dve.wait_ge(key_step[ph - 1], j * 3 + k)

                        key_done(vec.tensor_tensor(key[:, :], src_b[:, :], dst_rel[:, :], ALU.subtract), 1)
                        key_done(vec.scalar_tensor_tensor(key[:, :], dst_rel[:, :], -float(WINDOW), key[:, :],
                                                          ALU.is_gt, ALU.mult), 2)
                        key_done(vec.scalar_tensor_tensor(key[:, :], dst_rel[:, :], 0.0, key[:, :],
                                                          ALU.is_le, ALU.mult), 3)

                    def end(j, n, ph=ph):
                        left = 2 * UNIT - 1
                        for i, at in enumerate(load_bases(GROUPS - left, left)):
                            add_unit_window(at, (i + 1) % UNIT, n * UNIT + (i - left))
                        move_windows(ph, j)

                    over_units(dve, n_pass, nothing, unit, end, begin)
                    if ph == 1:
                        dve.wait_ge(inv_deg_in, 16)
                        for a in range(0, NODES, CHUNK):
                            z = min(a + CHUNK, NODES)
                            vec.tensor_tensor(stack[0:ROWS, a:z], stack[0:ROWS, a:z], inv_deg[:, a:z],
                                              ALU.mult).then_inc(mean_ready, 1)
                        vec.memset(acc[0:ROWS, :], 0.0)
                        done(vec.tensor_tensor(x[:, :, :], x[:, :, :],
                                               sage2_b[:, :].unsqueeze(1).to_broadcast([TILE, BLOCKS, FEAT]), ALU.add))
                        y = [(a, z, psum[:TILE, a // 4, 0:(z - a) * 128].rearrange("p (b f) -> p b f", f=128))
                             for a, z in ((a, min(a + 4, BLOCKS)) for a in range(0, BLOCKS, 4))]
                        for k, (a, z, got) in enumerate(y):
                            dve.wait_ge(y_summed, k + 1)
                            last = vec.tensor_copy(h[:, a:z, :], got[:, :, 0:FEAT])
                        last.then_inc(y_ready, 1)
                        for a, z, got in y:
                            last = vec.tensor_tensor(x[:, a:z, :], x[:, a:z, :], got[:, :, FEAT:2 * FEAT], ALU.add)
                        last.then_inc(y_left, 1)
                    else:
                        dve.wait_ge(table_in[2], 16)
                        for k in range(BLOCKS // TURNED):
                            a, z = k * TURNED, (k + 1) * TURNED
                            dve.wait_ge(sums_turned[1], k + 1)
                            done(vec.tensor_reduce(h[:, a:z, :], psum[:TILE, k, 0:TURNED * ROWS].rearrange(
                                "p (b k f) -> p b f k", b=TURNED, k=PARTS), AX_X, ALU.add))
                            done(vec.tensor_tensor(h[:, a:z, :], h[:, a:z, :], spread(inv[:, a:z], FEAT), ALU.mult))
                            last = vec.tensor_tensor(h[:, a:z, :], x[:, a:z, :], h[:, a:z, :], ALU.add)
                        last.then_inc(out_ready, 1)


def kernel(**inputs):
    import concourse.bacc as _bacc
    from concourse.bass_utils import run_bass_kernel_spmd as _run

    a = {k: np.asarray(v) for k, v in inputs.items()}
    order = [0, 2, 1, 3]
    w2 = np.concatenate([a["L0_gnn_W2"], a["L0_gnn_b2"][None]], axis=0).reshape(HID0 + 1, 4, MUL * MUL)[:, order]
    laid = {
        "x": a["x"],
        "src": a["src"].reshape(TILES, TILE).T,
        "dst_tiles": a["dst"].reshape(TILES, TILE).T,
        "dst_groups": a["dst"].reshape(GROUPS, GEDGES),
        "ef_t": a["edge_attr_32"].T,
        "sh": a["edge_attr_4"].reshape(TILES, TILE, 4).transpose(1, 0, 2),
        "w1": a["L0_gnn_W1"], "b1": a["L0_gnn_b1"].reshape(HID0, 1), "w2": w2.reshape(HID0 + 1, WCOLS),
        "si0": a["L0_gnn_si_w0"], "si1": a["L0_gnn_si_w1"],
        "sage1": np.concatenate([a["L1_gnn_W1_l"]] * PARTS + [a["L1_gnn_W1_r"]], axis=0),
        "sage1_b": a["L1_gnn_b1"].reshape(HID1, 1),
        "sage2": np.concatenate([a["L1_gnn_W2_l"], a["L1_gnn_W2_r"]], axis=1),
        "sage2_b": a["L1_gnn_b2"].reshape(1, FEAT),
        "const": constants(),
        "columns": np.arange(1, COUNTS + 1, dtype=np.int16).reshape(1, COUNTS),
    }
    nc = _bacc.Bacc("TRN2", target_bir_lowering=False, num_devices=1)
    arrays, args = {}, []
    for name, v in laid.items():
        v = np.ascontiguousarray(v)
        arrays[f"in_{name}_dram"] = v
        args.append(nc.dram_tensor(f"in_{name}_dram", v.shape, mybir.dt.from_np(v.dtype), kind="ExternalInput").ap())
    args.append(nc.dram_tensor("out_dram", (NODES, FEAT), F32, kind="ExternalOutput").ap())
    gnn(nc, *args)
    r = _run(nc, [arrays], core_ids=[0])
    return r.results[0]["out_dram"]
```
